# Optimizing a Trainium2 kernel written in Bass

```python
import numpy as np
import jax
import jax.numpy as jnp

def _softmax(x, axis=-1):
    return jax.nn.softmax(x, axis=axis)

def _gelu(x):
    return jax.nn.gelu(x, approximate=True)

def _silu(x):
    return jax.nn.silu(x)

def _sigmoid(x):
    return jax.nn.sigmoid(x)

def _layernorm(x, axis=-1, eps=1e-05):
    m = jnp.mean(x, axis=axis, keepdims=True)
    v = jnp.var(x, axis=axis, keepdims=True)
    return (x - m) / jnp.sqrt(v + eps)

def _scatter_add(tgt, idx, src, axis=0):
    return tgt.at[idx].add(src)

def _segment_sum(src, seg, n):
    return jax.ops.segment_sum(src, seg, n)
kernel_name = 'mk_adaln_ffn_d2_seqx_r8_380e8b'

def setup_inputs(seed: int=0):
    np.random.seed(seed)
    _w = jnp.asarray

    def _rec_inputs():
        import jax
        import jax.numpy as jnp
        _rk = jax.random.key(seed)
        x = -0.000125 + 0.9999 * jax.random.normal(jax.random.fold_in(_rk, 1), (128, 32, 512), jnp.float32)
        _lenS = 32 - jax.random.randint(jax.random.fold_in(_rk, 7), (128,), 0, max(1, 32 // 4) + 1, jnp.int32)
        _lenS2 = 32 - jax.random.randint(jax.random.fold_in(_rk, 8), (128,), 0, max(1, 32 // 4) + 1, jnp.int32)
        cond_128 = 0.0061147 + 1.02565 * jax.random.normal(jax.random.fold_in(_rk, 11), (128, 128), jnp.float32)
        fside_S_0 = -0.022604 + 0.987366 * jax.random.normal(jax.random.fold_in(_rk, 12), (32,), jnp.float32)
        return (x, cond_128, fside_S_0)
    x, cond_128, fside_S_0 = _rec_inputs()

    def _L0_cond_setup():
        import jax, jax.numpy as jnp
        import numpy as np
        K = 8
        T = 1.0
        D_EMBD = 128
        IN_C = 32
        OUT_C = 32
        BS = 32
        H = 512
        HID = 128
        key = jax.random.key(seed)
        ks = jax.random.split(key, 10)
        s = lambda fan_in: 1.0 / np.sqrt(fan_in)
        return {'x': jax.random.normal(ks[0], (BS, IN_C, H), dtype=jnp.float32), 'embedding': jax.random.normal(ks[1], (BS, D_EMBD), dtype=jnp.float32), 'W0': jax.random.normal(ks[2], (D_EMBD, HID), dtype=jnp.float32) * s(D_EMBD), 'b0': jnp.zeros((HID,), dtype=jnp.float32), 'W1': jax.random.normal(ks[3], (HID, HID), dtype=jnp.float32) * s(HID), 'b1': jnp.zeros((HID,), dtype=jnp.float32), 'W2': jax.random.normal(ks[4], (HID, K), dtype=jnp.float32) * s(HID), 'b2': jnp.zeros((K,), dtype=jnp.float32), 'weight': jax.random.normal(ks[5], (K, OUT_C, IN_C, 1), dtype=jnp.float32) * s(IN_C), 'bias_k': jax.random.normal(ks[6], (K, OUT_C), dtype=jnp.float32) * 0.1}
    _L0_cond_all = _L0_cond_setup()
    _L0_cond_in = {k: v for k, v in _L0_cond_all.items() if k in ('W0', 'b0', 'W1', 'b1', 'W2', 'b2', 'weight', 'bias_k')}
    del _L0_cond_all

    def _L0_ffn_setup():
        import jax, jax.numpy as jnp
        import numpy as np
        SCALING = 16.0 / 8.0
        GAMMA = 1.0
        EPS = 1e-12
        key = jax.random.key(seed)
        ks = jax.random.split(key, 8)
        B, T, H, O = (4, 256, 512, 512)
        E_tot, E_act, r = (16, 4, 8)
        return {'x': jax.random.normal(ks[0], (B, T, H), jnp.float32), 'W_base': jax.random.normal(ks[1], (O, H), jnp.float32) * 0.02, 'b_base': jax.random.normal(ks[2], (O,), jnp.float32) * 0.02, 'lora_A': jax.random.normal(ks[3], (E_tot, r, H), jnp.float32) * 0.02, 'lora_B': jax.random.normal(ks[4], (E_tot, O, r), jnp.float32) * 0.02, 'router_W': jax.random.normal(ks[5], (E_tot, H), jnp.float32) * 0.02, 'router_b': jax.random.normal(ks[6], (E_tot,), jnp.float32) * 0.02, 'domain_prior': jax.random.uniform(ks[7], (E_tot,), jnp.float32), 'active': jnp.arange(E_act, dtype=jnp.int32)}
    _L0_ffn_all = _L0_ffn_setup()
    _L0_ffn_in = {k: v for k, v in _L0_ffn_all.items() if k in ('W_base', 'b_base', 'lora_A', 'lora_B', 'router_W', 'router_b', 'domain_prior', 'active')}
    del _L0_ffn_all

    def _L1_cond_setup():
        import jax, jax.numpy as jnp
        import numpy as np
        from jax import lax
        N, C_IN, L = (32, 32, 512)
        C_OUT, K, GROUPS = (32, 9, 4)
        C_DIM, PAD, STRIDE = (128, 4, 1)
        key = jax.random.key(seed)
        k1, k2, k3, k4, k5 = jax.random.split(key, 5)
        x = jax.random.normal(k1, (N, C_IN, L), dtype=jnp.float32)
        c = jax.random.normal(k2, (N, C_DIM), dtype=jnp.float32)
        weight = jax.random.normal(k3, (C_OUT, C_IN // GROUPS, K), dtype=jnp.float32)
        c_weight = jax.random.normal(k4, (C_OUT, C_DIM), dtype=jnp.float32)
        bias = jax.random.normal(k5, (C_OUT,), dtype=jnp.float32)
        return {'x': x, 'c': c, 'weight': weight, 'c_weight': c_weight, 'bias': bias}
    _L1_cond_all = _L1_cond_setup()
    _L1_cond_in = {k: v for k, v in _L1_cond_all.items() if k in ('weight', 'c_weight')}
    del _L1_cond_all

    def _L1_ffn_setup():
        import jax, jax.numpy as jnp
        import numpy as np
        N_EXPERTS = 28
        TOP_K = 2
        RANK = 8
        LORA_ALPHA = 16
        SCALING = LORA_ALPHA / RANK
        TEMP = 1.0
        key = jax.random.key(seed)
        ks = jax.random.split(key, 5)
        B, S, D_IN, D_OUT = (4, 256, 512, 512)
        x = jax.random.normal(ks[0], (B, S, D_IN), dtype=jnp.float32)
        base_W = jax.random.normal(ks[1], (D_OUT, D_IN), dtype=jnp.float32) * (1.0 / np.sqrt(D_IN))
        gate_W = jax.random.normal(ks[2], (N_EXPERTS, D_IN), dtype=jnp.float32) * (1.0 / np.sqrt(D_IN))
        lora_A = jax.random.normal(ks[3], (N_EXPERTS, RANK, D_IN), dtype=jnp.float32) * (1.0 / np.sqrt(D_IN))
        lora_B = jax.random.normal(ks[4], (N_EXPERTS, D_OUT, RANK), dtype=jnp.float32) * 0.01
        return {'x': x, 'base_W': base_W, 'gate_W': gate_W, 'lora_A': lora_A, 'lora_B': lora_B}
    _L1_ffn_all = _L1_ffn_setup()
    _L1_ffn_in = {k: v for k, v in _L1_ffn_all.items() if k in ('base_W', 'gate_W', 'lora_A', 'lora_B')}
    del _L1_ffn_all
    return {'x': x, 'cond_128': cond_128, 'fside_S_0': fside_S_0, 'L0_cond_W0': _L0_cond_in['W0'], 'L0_cond_b0': _L0_cond_in['b0'], 'L0_cond_W1': _L0_cond_in['W1'], 'L0_cond_b1': _L0_cond_in['b1'], 'L0_cond_W2': _L0_cond_in['W2'], 'L0_cond_b2': _L0_cond_in['b2'], 'L0_cond_weight': _L0_cond_in['weight'], 'L0_cond_bias_k': _L0_cond_in['bias_k'], 'L0_ffn_W_base': _L0_ffn_in['W_base'], 'L0_ffn_b_base': _L0_ffn_in['b_base'], 'L0_ffn_lora_A': _L0_ffn_in['lora_A'], 'L0_ffn_lora_B': _L0_ffn_in['lora_B'], 'L0_ffn_router_W': _L0_ffn_in['router_W'], 'L0_ffn_router_b': _L0_ffn_in['router_b'], 'L0_ffn_domain_prior': _L0_ffn_in['domain_prior'], 'L0_ffn_active': _L0_ffn_in['active'], 'L1_cond_weight': _L1_cond_in['weight'], 'L1_cond_c_weight': _L1_cond_in['c_weight'], 'L1_ffn_base_W': _L1_ffn_in['base_W'], 'L1_ffn_gate_W': _L1_ffn_in['gate_W'], 'L1_ffn_lora_A': _L1_ffn_in['lora_A'], 'L1_ffn_lora_B': _L1_ffn_in['lora_B']}

def reference(x, cond_128, fside_S_0, L0_cond_W0, L0_cond_b0, L0_cond_W1, L0_cond_b1, L0_cond_W2, L0_cond_b2, L0_cond_weight, L0_cond_bias_k, L0_ffn_W_base, L0_ffn_b_base, L0_ffn_lora_A, L0_ffn_lora_B, L0_ffn_router_W, L0_ffn_router_b, L0_ffn_domain_prior, L0_ffn_active, L1_cond_weight, L1_cond_c_weight, L1_ffn_base_W, L1_ffn_gate_W, L1_ffn_lora_A, L1_ffn_lora_B):
    import jax
    import jax.numpy as jnp

    def _L0_cond_ref(x, embedding, W0, b0, W1, b1, W2, b2, weight, bias_k):
        import jax, jax.numpy as jnp
        import numpy as np
        K = 8
        T = 1.0
        D_EMBD = 128
        IN_C = 32
        OUT_C = 32
        BS = 32
        H = 512
        HID = 128
        h = jax.nn.gelu(embedding @ W0 + b0, approximate=False)
        h = jax.nn.gelu(h @ W1 + b1, approximate=False)
        att = jax.nn.softmax((h @ W2 + b2) / T, axis=-1)
        agg_w = jnp.einsum('bk,koi->boi', att, weight[..., 0])
        agg_b = att @ bias_k
        out = jnp.einsum('boi,bih->boh', agg_w, x) + agg_b[:, :, None]
        return out

    def _L0_ffn_ref(x, W_base, b_base, lora_A, lora_B, router_W, router_b, domain_prior, active):
        import jax, jax.numpy as jnp
        import numpy as np
        SCALING = 16.0 / 8.0
        GAMMA = 1.0
        EPS = 1e-12
        y = jnp.einsum('bth,oh->bto', x, W_base) + b_base
        A = lora_A[active]
        Bm = lora_B[active]
        z = jnp.einsum('bth,erh->bter', x, A)
        contribs = jnp.einsum('bter,eor->bteo', z, Bm) * SCALING
        logits = jnp.einsum('bth,eh->bte', x, router_W) + router_b
        logits = logits[..., active]
        prior = domain_prior[active]
        alpha = jax.nn.softmax(jnp.log(prior + EPS) + logits / GAMMA, axis=-1)
        return y + jnp.einsum('bteo,bte->bto', contribs, alpha)

    def _L1_cond_ref(x, c, weight, c_weight, bias):
        import jax, jax.numpy as jnp
        import numpy as np
        from jax import lax
        N, C_IN, L = (32, 32, 512)
        C_OUT, K, GROUPS = (32, 9, 4)
        C_DIM, PAD, STRIDE = (128, 4, 1)
        out = lax.conv_general_dilated(x, weight, window_strides=(STRIDE,), padding=[(PAD, PAD)], dimension_numbers=('NCH', 'OIH', 'NCH'), feature_group_count=GROUPS)
        ctx = jnp.einsum('nd,od->no', c, c_weight)
        out = out + ctx[:, :, None] + bias[None, :, None]
        return out

    def _L1_ffn_ref(x, base_W, gate_W, lora_A, lora_B):
        import jax, jax.numpy as jnp
        import numpy as np
        N_EXPERTS = 28
        TOP_K = 2
        RANK = 8
        LORA_ALPHA = 16
        SCALING = LORA_ALPHA / RANK
        TEMP = 1.0
        B, S, D_in = x.shape
        xf = x.reshape(B * S, D_in)
        base = xf @ base_W.T
        logits = xf @ gate_W.T
        top_vals, top_idx = jax.lax.top_k(logits, TOP_K)
        top_probs = jax.nn.softmax(top_vals / TEMP, axis=-1)
        N = xf.shape[0]
        gate_full = jnp.zeros((N, N_EXPERTS), dtype=xf.dtype).at[jnp.arange(N)[:, None], top_idx].add(top_probs)
        h = jnp.einsum('nd,erd->ner', xf, lora_A)
        h = h * (gate_full * SCALING)[:, :, None]
        lora_out = jnp.einsum('ner,eor->no', h, lora_B)
        out = base + lora_out
        return out.reshape(B, S, -1)
    x = x + _L0_ffn_ref(_L0_cond_ref(x, cond_128, L0_cond_W0, L0_cond_b0, L0_cond_W1, L0_cond_b1, L0_cond_W2, L0_cond_b2, L0_cond_weight, L0_cond_bias_k), L0_ffn_W_base, L0_ffn_b_base, L0_ffn_lora_A, L0_ffn_lora_B, L0_ffn_router_W, L0_ffn_router_b, L0_ffn_domain_prior, L0_ffn_active)
    x = x + _L1_ffn_ref(_L1_cond_ref(x, cond_128, L1_cond_weight, L1_cond_c_weight, fside_S_0), L1_ffn_base_W, L1_ffn_gate_W, L1_ffn_lora_A, L1_ffn_lora_B)
    return x

_drawn_inputs = setup_inputs


def setup_inputs(seed=0):
    import zlib

    import numpy as np

    out = dict(_drawn_inputs(seed))
    spreads = {'L0_cond_b0': (0.0, 0.8), 'L0_cond_b1': (0.0, 0.8), 'L0_cond_b2': (0.0, 0.8)}
    factors = {'L0_cond_bias_k': 6.129,
     'L0_ffn_b_base': 4.616,
     'L0_ffn_lora_A': 7.996,
     'L0_ffn_lora_B': 7.983,
     'L0_ffn_router_W': 8.0,
     'L0_ffn_router_b': 8.0,
     'L0_ffn_domain_prior': 8.0}
    for name, (base, spread) in spreads.items():
        noise = np.random.default_rng([zlib.crc32(name.encode()), seed]).standard_normal(out[name].shape)
        drawn = base * np.exp(spread * noise) if base else spread * noise
        out[name] = jnp.asarray(drawn.astype(out[name].dtype))
    for name, factor in factors.items():
        out[name] = (out[name] * factor).astype(out[name].dtype)
    return out
```

```python
import numpy as np

import concourse.bass as bass
from concourse import mybir
from contextlib import ExitStack

P = 128
BATCH, CH, D = 128, 32, 512
BT = P // CH
NT = BATCH // BT
HC = D // P
NPH, NQ = 4, D // 4
GROUPS, GC, TAPS = 4, 8, 9
CG = BT * GROUPS
WIN = 12
KIM = WIN * GC
NQP = NQ + 2
E0, ACT0, R = 16, 4, 8
L0N = ACT0 * R
Z0N = L0N + ACT0
E1 = 28
L1N = E1 * R
H1N = L1N + E1
HB = L1N // 2
K1 = HB + 1
K0 = 3 * L0N + 5
MK = 8
SCALING = 2.0
EPS = 1e-12
UNROLL, LAG = 4, 2

C_COND, C_W0, C_W1, C_W2, C_B2, C_B0, C_B1, C_FS, C_CW = 0, 128, 256, 384, 392, 400, 401, 402, 403
C_END = C_CW + CH


class Tile:

    def __init__(self, i, c):
        self.i, self.c = i, c

    def __add__(self, n):
        return Tile(self.i, self.c + n)

    def n(self):
        return self.c if self.i is None else self.i * UNROLL + self.c

    def mod(self, m):
        return self.c % m

    def over(self, m):
        return self.c // m if self.i is None else self.i * (UNROLL // m) + self.c // m

    def live(self):
        return self.i is not None or 0 <= self.c < NT


def steps(engine, step, first, last, loop_from, loops):
    for c in range(first, loop_from):
        step(Tile(None, c))
    with engine.Fori(0, loops) as i:
        for u in range(UNROLL):
            step(Tile(i, loop_from + u))
    for c in range(loop_from + loops * UNROLL, last + 1):
        step(Tile(None, c))


def build(nc, x, pack, kw, experts, router, active, b_base, w0, w1, a1, b1, wc, out):
    f32, f32r, i32, u32 = mybir.dt.float32, mybir.dt.float32r, mybir.dt.int32, mybir.dt.uint32
    ALU = mybir.AluOpType
    ACT = mybir.ActivationFunctionType
    X = mybir.AxisListType.X

    ctx = ExitStack()
    with ctx:
        def sb(name, shape, dt=f32):
            return ctx.enter_context(nc.sbuf_tensor(name, shape, dt))

        def pb(name):
            return ctx.enter_context(nc.psum_tensor(name, [P, 512], f32))

        def sem(name):
            return ctx.enter_context(nc.semaphore(name))

        scratch = nc.dram_tensor("x1_scratch", (NT, P, NPH, NQP), f32, kind="Internal").ap()

        pack_sb = sb("pack_sb", [P, C_END])
        kw_sb = sb("kw_sb", [BT * MK, CH + 1, P])
        exp_sb = sb("exp_sb", [P, 2, D])
        rt_sb = sb("rt_sb", [E0, D + 2])
        act_sb = sb("act_sb", [P, ACT0], i32)
        bb_sb = sb("bb_sb", [1, D])
        w_sb = sb("w_sb", [P, 2, HC, D])
        a1_sb = sb("a1_sb", [P, HC, H1N])
        b1_sb = sb("b1_sb", [HB, 2, D])
        wc_sb = sb("wc_sb", [KIM, GROUPS, NPH * GC])
        w_hi = sb("w_hi", [P, 2, HC, D], f32r)
        w_lo = sb("w_lo", [P, 2, HC, D], f32r)
        a0_hi = sb("a0_hi", [P, HC, Z0N], f32r)
        a0_lo = sb("a0_lo", [P, HC, Z0N], f32r)
        a1_hi = sb("a1_hi", [P, HC, H1N], f32r)
        a1_lo = sb("a1_lo", [P, HC, H1N], f32r)
        b0_round = sb("b0_round", [K0, D], f32r)
        b0_stack = sb("b0_stack", [K0, D], f32r)
        b1_hi = sb("b1_hi", [K1, 2, D], f32r)
        b1_lo = sb("b1_lo", [K1, 2, D], f32r)
        mix_hi = sb("mix_hi", [P, NT, P], f32r)
        mix_lo = sb("mix_lo", [P, NT, P], f32r)

        ident = sb("ident", [P, P])
        ones_r = sb("ones_r", [P, P], f32r)
        pick_rs0 = sb("pick_rs0", [P, K0], f32r)
        pick_bias = sb("pick_bias", [1, K0])
        pick_rs1 = sb("pick_rs1", [P, K1], f32r)
        minus_lo_row = sb("minus_lo_row", [P, 1])
        iota_slot = sb("iota_slot", [P, ACT0, R], i32)
        iota_row = sb("iota_row", [E0, ACT0], i32)
        iota_e_i = sb("iota_e_i", [P, E1], i32)
        iota_e = sb("iota_e", [P, E1])
        act8 = sb("act8", [P, ACT0])
        sel = sb("sel", [P, K0])
        sel_r = sb("sel_r", [E0, ACT0])
        mask_c = sb("mask_c", [P, BT])
        mask_t = sb("mask_t", [P, NT])

        m1 = sb("m1", [P, BATCH])
        m2 = sb("m2", [P, BATCH])
        am = sb("am", [P, MK])
        am_max = sb("am_max", [P, 1])
        am_exp = sb("am_exp", [P, MK])
        am_sum = sb("am_sum", [P, 1])
        am_rec = sb("am_rec", [P, 1])
        att = sb("att", [P, MK])
        att_m = sb("att_m", [P, BT, MK])
        att_t = sb("att_t", [BT * MK, NT])
        beta0 = sb("beta0", [P, NT])
        beta1 = sb("beta1", [P, NT])
        beta5 = sb("beta5", [P, NT, 5])
        rs0 = sb("rs0", [P, Z0N])
        vcol = sb("vcol", [E0, 1])
        vcol2 = sb("vcol2", [E0, 1])
        vmat = sb("vmat", [E0, P])
        vrow = sb("vrow", [P, ACT0])
        z_add = sb("z_add", [P, NT, Z0N])
        rs1 = sb("rs1", [P, H1N])

        x_sb = sb("x_sb", [P, 4, D])
        x_hi = sb("x_hi", [P, 2, D], f32r)
        x_lo = sb("x_lo", [P, 2, D], f32r)
        c0_hi = sb("c0_hi", [P, D], f32r)
        c0_lo = sb("c0_lo", [P, D], f32r)
        z0 = sb("z0", [P, Z0N])
        z0_nmax = sb("z0_nmax", [P, 1])
        z0_exp = sb("z0_exp", [P, ACT0])
        z0_sum = sb("z0_sum", [P, 1])
        z0_rec = sb("z0_rec", [P, 1])
        alpha = sb("alpha", [P, ACT0])
        g0 = sb("g0", [P, L0N])
        g0s = sb("g0s", [P, K0])
        g0t = sb("g0t", [K0, P], f32r)
        x1 = sb("x1", [P, 4, NPH, NQP])
        win = sb("win", [KIM, 2, CG, NQ])
        c1_hi = sb("c1_hi", [P, NPH, P], f32r)
        c1_lo = sb("c1_lo", [P, NPH, P], f32r)
        h1 = sb("h1", [P, H1N])
        top = sb("top", [P, 8])
        top_i = sb("top_i", [P, 8], u32)
        top_f = sb("top_f", [P, 2])
        ntop = sb("ntop", [P, 1])
        t_exp = sb("t_exp", [P, 2])
        t_sum = sb("t_sum", [P, 1])
        t_rec = sb("t_rec", [P, 1])
        prob = sb("prob", [P, 2])
        gate_a = sb("gate_a", [P, E1])
        gate_b = sb("gate_b", [P, E1])
        gate = sb("gate", [P, E1])
        g1 = sb("g1", [P, 2, K1])
        g1t_hi = sb("g1t_hi", [K1, 2, P], f32r)
        g1t_lo = sb("g1t_lo", [K1, 2, P], f32r)
        y_sb = sb("y_sb", [P, 2, D])

        p_c0, p_y0, p_z0, p_g0 = pb("p_c0"), pb("p_y0"), pb("p_z0"), pb("p_g0")
        p_c1, p_y1, p_h1, p_g1 = pb("p_c1"), pb("p_y1"), pb("p_h1"), pb("p_g1")

        ld_pack, ld_kw, ld_exp, ld_rt = sem("ld_pack"), sem("ld_kw"), sem("ld_exp"), sem("ld_rt")
        ld_act, ld_bb, ld_w0, ld_w1 = sem("ld_act"), sem("ld_bb"), sem("ld_w0"), sem("ld_w1")
        ld_a1, ld_b1, ld_wc = sem("ld_a1"), sem("ld_b1"), sem("ld_wc")
        x_loaded = [sem(f"x_loaded{n}") for n in range(4)]
        x1_stored = [sem(f"x1_stored{n}") for n in range(4)]
        win_loaded = [sem(f"win_loaded{n}") for n in range(2)]
        y_stored = [sem(f"y_stored{n}") for n in range(2)]

        zeroed_id, ident_done, ones_done, picks_zeroed = sem("zeroed_id"), sem("ident_done"), sem("ones_done"), sem("picks_zeroed")
        picks_done, iotas_done, mix_zeroed, x1_padded = sem("picks_done"), sem("iotas_done"), sem("mix_zeroed"), sem("x1_padded")
        g1_padded, lomask_0, lomask_1, lomask_2, lomask_done = sem("g1_padded"), sem("lomask_0"), sem("lomask_1"), sem("lomask_2"), sem("lomask_done")
        masks_done, u1_mm, m1_done = sem("masks_done"), sem("u1_mm"), sem("m1_done")
        u2_mm, m2_done = sem("u2_mm"), sem("m2_done")
        am_mm, am_done, am_max_done, am_exp_done = sem("am_mm"), sem("am_done"), sem("am_max_done"), sem("am_exp_done")
        am_rec_done, att_done, att_m_done, att_t_mm, att_t_done = sem("am_rec_done"), sem("att_done"), sem("att_m_done"), sem("att_t_mm"), sem("att_t_done")
        beta1_mm, beta1_done, beta0_mm, beta0_done = sem("beta1_mm"), sem("beta1_done"), sem("beta0_mm"), sem("beta0_done")
        mix_mm, mix_hi_done, mix_lo_done = sem("mix_mm"), sem("mix_hi_done"), sem("mix_lo_done")
        iota_e_done, act8_done, sel_zeroed, sel_done, sel_r_done = sem("iota_e_done"), sem("act8_done"), sem("sel_zeroed"), sem("sel_done"), sem("sel_r_done")
        a0_mm, a0_hi_done, a0_lo_done = sem("a0_mm"), sem("a0_hi_done"), sem("a0_lo_done")
        w_hi_done, w_lo_done = sem("w_hi_done"), sem("w_lo_done")
        a1_hi_done, a1_lo_done = sem("a1_hi_done"), sem("a1_lo_done")
        b0_mm, b0_round_done, b0_done = sem("b0_mm"), sem("b0_round_done"), sem("b0_done")
        b1_mm, b1_hi_done, b1_lo_done = sem("b1_mm"), sem("b1_hi_done"), sem("b1_lo_done")
        rs0_mm, rs0_done, vlog_done, vcol2_done, vmat_done = sem("rs0_mm"), sem("rs0_done"), sem("vlog_done"), sem("vcol2_done"), sem("vmat_done")
        vrow_mm, vrow_done, z_mul_done, z_add_done = sem("vrow_mm"), sem("vrow_done"), sem("z_mul_done"), sem("z_add_done")
        rs1_mm, rs1_done = sem("rs1_mm"), sem("rs1_done")
        beta5_ones, beta5_hi, beta5_lo, beta5_done = sem("beta5_ones"), sem("beta5_hi"), sem("beta5_lo"), sem("beta5_done")
        eps_done = sem("eps_done")

        x_hi_done, x_lo_done = sem("x_hi_done"), sem("x_lo_done")
        c0_mm, c0_hi_done, c0_lo_done = sem("c0_mm"), sem("c0_hi_done"), sem("c0_lo_done")
        z0_mm, z0_done, z0_nmax_done, z0_exp_done = sem("z0_mm"), sem("z0_done"), sem("z0_nmax_done"), sem("z0_exp_done")
        z0_rec_done, alpha_done, g0_done, g0_hi_done = sem("z0_rec_done"), sem("alpha_done"), sem("g0_done"), sem("g0_hi_done")
        g0_lo_done, g0_beta_done = sem("g0_lo_done"), sem("g0_beta_done")
        g0_tr, g0t_done, y0_mm, x1_done = sem("g0_tr"), sem("g0t_done"), sem("y0_mm"), sem("x1_done")
        c1_mm, c1_hi_done, c1_lo_done = sem("c1_mm"), sem("c1_hi_done"), sem("c1_lo_done")
        h1_mm, logits_done, h1_done, top_done, top_i_done, ntop_done = sem("h1_mm"), sem("logits_done"), sem("h1_done"), sem("top_done"), sem("top_i_done"), sem("ntop_done")
        top_f_done, t_exp_done, t_rec_done, prob_done = sem("top_f_done"), sem("t_exp_done"), sem("t_rec_done"), sem("prob_done")
        gate_a_done, gate_b_done, gate_done, g1_done, g1_beta_done = sem("gate_a_done"), sem("gate_b_done"), sem("gate_done"), sem("g1_done"), sem("g1_beta_done")
        g1_tr, g1t_hi_done, g1t_lo_done = sem("g1_tr"), sem("g1t_hi_done"), sem("g1t_lo_done")
        y1_mm, y_done = sem("y1_mm"), sem("y_done")

        x_v = x.rearrange("(t b) c h -> t (b c) h", b=BT)
        out_v = out.rearrange("(t b) c h -> t (b c) h", b=BT)
        scr_w = scratch

        block = ctx.enter_context(nc.Block())

        def after(eng, semaphore, tile, ahead=0):
            t = tile + ahead
            if t.i is None and t.c < 0:
                return
            eng.wait_ge(semaphore, t.n() + 1)

        def after_dma(eng, semaphores, tile, ahead=0, count=16):
            t = tile + ahead
            if t.i is None and t.c < 0:
                return
            m = len(semaphores)
            eng.wait_ge(semaphores[t.mod(m)], (t.over(m) + 1) * count)

        @block.sync
        def _(sp):
            sp.dma_start(pack_sb[:], pack).then_inc(ld_pack, 16)
            sp.dma_start(act_sb[:], active).then_inc(ld_act, 16)
            sp.dma_start(kw_sb[:], kw.rearrange("k (o p) -> k o p", p=P)).then_inc(ld_kw, 16)
            sp.dma_start(x_sb[:, 0, :], x_v[0]).then_inc(x_loaded[0], 16)
            sp.dma_start(exp_sb[:], experts.rearrange("p (a d) -> p a d", a=2)).then_inc(ld_exp, 16)
            sp.dma_start(rt_sb[:], router).then_inc(ld_rt, 16)
            sp.dma_start(w_sb[:, 0], w0.rearrange("p (c d) -> p c d", c=HC)).then_inc(ld_w0, 16)
            sp.dma_start(bb_sb[:], b_base).then_inc(ld_bb, 16)
            sp.dma_start(x_sb[:, 1, :], x_v[1]).then_inc(x_loaded[1], 16)
            sp.dma_start(a1_sb[:], a1.rearrange("p (c n) -> p c n", c=HC)).then_inc(ld_a1, 16)
            sp.dma_start(w_sb[:, 1], w1.rearrange("p (c d) -> p c d", c=HC)).then_inc(ld_w1, 16)
            sp.dma_start(wc_sb[:], wc.rearrange("k (g n) -> k g n", g=GROUPS)).then_inc(ld_wc, 16)
            sp.dma_start(b1_sb[:], b1.rearrange("p (a d) -> p a d", a=2)).then_inc(ld_b1, 16)

            def step(s):
                if (s + -1).live():
                    v = s + -1
                    after_dma(sp, x1_stored, v)
                    after(sp, c1_mm, v, -2)
                    sv = scratch[v.n()].rearrange("(cg i) f q -> i f cg q", i=GC)
                    for j in range(3):
                        for f in range(NPH):
                            r0 = (j * NPH + f) * GC
                            sp.dma_start(win[r0:r0 + GC, v.mod(2)], sv[:, f, :, j:j + NQ]).then_inc(win_loaded[v.mod(2)], 16)
                if (s + 2).live() and (s.i is not None or s.c >= 0):
                    after(sp, x1_done, s, -2)
                    sp.dma_start(x_sb[:, (s + 2).mod(4), :], x_v[(s + 2).n()]).then_inc(x_loaded[(s + 2).mod(4)], 16)
                if (s + -3).live():
                    v = s + -3
                    after(sp, y_done, v)
                    sp.dma_start(out_v[v.n()], y_sb[:, v.mod(2), :]).then_inc(y_stored[v.mod(2)], 16)
                if s.live():
                    after(sp, x1_done, s)
                    sp.dma_start(scratch[s.n()], x1[:, s.mod(4)]).then_inc(x1_stored[s.mod(4)], 16)

            steps(sp, step, 0, NT + 2, 3, 6)
            for n in range(2):
                sp.wait_ge(y_stored[n], 16 * NT // 2)

        @block.gpsimd
        def _(pool):
            pool.memset(ident[:], 0.0).then_inc(zeroed_id, 1)
            pool.wait_ge(zeroed_id, 1)
            pool.affine_select(out=ident[:], in_=ident[:], compare_op=ALU.not_equal, fill=1.0, base=0,
                               pattern=[[-1, P]], channel_multiplier=1).then_inc(ident_done, 1)
            pool.iota(iota_slot[:], pattern=[[0, ACT0], [-1, R]], base=0, channel_multiplier=1).then_inc(iotas_done, 1)
            pool.iota(iota_row[:], pattern=[[0, ACT0]], base=0, channel_multiplier=1).then_inc(iotas_done, 1)
            pool.iota(iota_e_i[:], pattern=[[1, E1]], base=0, channel_multiplier=0).then_inc(iotas_done, 1)
            pool.memset(minus_lo_row[:], 0.0).then_inc(lomask_0, 1)
            pool.wait_ge(lomask_0, 1)
            pool.memset(minus_lo_row[2 * L0N:3 * L0N], -1.0).then_inc(lomask_1, 1)
            pool.wait_ge(lomask_1, 1)
            pool.affine_select(out=minus_lo_row[:], in_=minus_lo_row[:], compare_op=ALU.not_equal, fill=-1.0,
                               base=-(3 * L0N + 2), pattern=[[0, 1]], channel_multiplier=1).then_inc(lomask_2, 1)
            pool.wait_ge(lomask_2, 1)
            pool.affine_select(out=minus_lo_row[:], in_=minus_lo_row[:], compare_op=ALU.not_equal, fill=-1.0,
                               base=-(3 * L0N + 4), pattern=[[0, 1]], channel_multiplier=1).then_inc(lomask_done, 1)
            pool.memset(mix_hi[:].bitcast(f32), 0.0).then_inc(mix_zeroed, 1)
            pool.memset(mix_lo[:].bitcast(f32), 0.0).then_inc(mix_zeroed, 1)
            pool.memset(g1[:, 0, HB:K1], 0.0).then_inc(g1_padded, 1)
            for f in range(2):
                pool.memset(x1[:, :, :, f * (NQP - 1):f * (NQP - 1) + 1], 0.0).then_inc(x1_padded, 1)

            def step(s):
                if (s + 1).live():
                    t = s + 1
                    after(pool, x_hi_done, t)
                    pool.tensor_tensor(x_lo[:, t.mod(2), :], x_sb[:, t.mod(4), :],
                                       x_hi[:, t.mod(2), :].bitcast(f32), ALU.subtract).then_inc(x_lo_done, 1)
                if s.live():
                    if s.i is None and s.c == 0:
                        pool.wait_ge(beta5_done, 1)
                    after(pool, g0_tr, s, -1)
                    pool.tensor_copy(g0s[:, 3 * L0N:K0], beta5[:, s.n(), :]).then_inc(g0_beta_done, 1)
                if (s + -LAG).live():
                    v = s + -LAG
                    if v.i is None and v.c == 0:
                        pool.wait_ge(beta1_done, BT)
                    after(pool, g1_tr, v, -1)
                    pool.tensor_copy(g1[:, 1, HB:K1], beta1[:, bass.ds(v.n(), 1)]).then_inc(g1_beta_done, 1)

            steps(pool, step, -1, NT + 1, 3, 7)

        @block.scalar
        def _(act):
            act.wait_ge(ld_pack, 16)
            act.wait_ge(u1_mm, 1)
            nc.scalar.activation(m1[:], p_c0[:, 0:P], ACT.Gelu, bias=pack_sb[:, C_B0:C_B0 + 1]).then_inc(m1_done, 1)
            act.wait_ge(u2_mm, 1)
            nc.scalar.activation(m2[:], p_c0[:, 0:P], ACT.Gelu, bias=pack_sb[:, C_B1:C_B1 + 1]).then_inc(m2_done, 1)
            act.wait_ge(eps_done, 1)
            nc.scalar.activation(vcol[:], vcol2[:], ACT.Ln).then_inc(vlog_done, 1)
            act.wait_ge(am_max_done, 1)
            nc.scalar.activation(am_exp[:], am[:], ACT.Exp, bias=am_max[:], accum_out=am_sum[:]).then_inc(am_exp_done, 1)
            act.wait_ge(x_loaded[0], 16)
            nc.scalar.copy(x_hi[:, 0, :], x_sb[:, 0, :]).then_inc(x_hi_done, 1)
            act.wait_ge(ld_w0, 16)
            nc.scalar.copy(w_hi[:, 0], w_sb[:, 0]).then_inc(w_hi_done, 1)
            act.wait_ge(a0_mm, 1)
            nc.scalar.copy(a0_hi[:], p_h1[:, 0:HC * Z0N].rearrange("p (c n) -> p c n", c=HC)).then_inc(a0_hi_done, 1)
            act.wait_ge(mix_mm, 1)
            act.wait_ge(mix_zeroed, 2)
            for b in range(BT):
                for h, bank in enumerate((p_c1, p_y1)):
                    rows = slice(b * CH, (b + 1) * CH)
                    nc.scalar.copy(mix_hi[rows, :, b * CH + 16 * h:b * CH + 16 * h + 16],
                                   bank[rows, :].rearrange("p (o t) -> p t o", t=NT)).then_inc(mix_hi_done, 1)
            act.wait_ge(b0_mm, 1)
            nc.scalar.copy(b0_round[:], p_y0[0:K0, :]).then_inc(b0_round_done, 1)

            def step(s):
                if (s + 1).live() and (s.i is not None or s.c >= 0):
                    t = s + 1
                    after_dma(act, x_loaded, t)
                    after(act, c0_mm, t, -2)
                    nc.scalar.copy(x_hi[:, t.mod(2), :], x_sb[:, t.mod(4), :]).then_inc(x_hi_done, 1)
                if s.live():
                    after(act, z0_nmax_done, s)
                    nc.scalar.activation(z0_exp[:], z0[:, L0N:Z0N], ACT.Exp, bias=z0_nmax[:],
                                         accum_out=z0_sum[:]).then_inc(z0_exp_done, 1)
                if (s + -3).live():
                    after(act, g1_tr, s, -3)
                    nc.scalar.copy(g1t_hi[:], p_g1[0:K1, 0:2 * P].rearrange("p (a n) -> p a n", a=2)).then_inc(g1t_hi_done, 1)
                if (s + -LAG).live():
                    after(act, c1_mm, s, -LAG)
                    nc.scalar.copy(c1_hi[:].rearrange("p r (a o) -> p a r o", o=GC),
                                   p_c1[:].rearrange("p (a r o) -> p a r o", r=NPH, o=GC)).then_inc(c1_hi_done, 1)
                if s.live():
                    after(act, g0_tr, s)
                    nc.scalar.copy(g0t[:], p_g0[0:K0, 0:P]).then_inc(g0t_done, 1)
                if (s + 1).live():
                    after(act, c0_mm, s, 1)
                    nc.scalar.copy(c0_hi[:], p_c0[:]).then_inc(c0_hi_done, 1)
                if s.i is None and s.c == 0:
                    act.wait_ge(ld_a1, 16)
                    nc.scalar.copy(a1_hi[:], a1_sb[:]).then_inc(a1_hi_done, 1)
                    act.wait_ge(ld_w1, 16)
                    nc.scalar.copy(w_hi[:, 1], w_sb[:, 1]).then_inc(w_hi_done, 1)
                if s.i is None and s.c == 1:
                    for a in range(2):
                        act.wait_ge(b1_mm, a + 1)
                        nc.scalar.copy(b1_hi[:, a, :], (p_g1, p_h1)[a][0:K1, :]).then_inc(b1_hi_done, 1)
                if (s + -LAG).live():
                    after(act, ntop_done, s, -LAG)
                    nc.scalar.activation(t_exp[:], top[:, 0:2], ACT.Exp, bias=ntop[:],
                                         accum_out=t_sum[:]).then_inc(t_exp_done, 1)

            steps(act, step, -1, NT + 2, 3, 7)

        @block.vector
        def _(dve):
            V = nc.vector
            dve.wait_ge(ld_pack, 16)
            dve.wait_ge(ident_done, 1)
            V.tensor_reduce(mask_c[:], ident[:].rearrange("p (t c) -> p c t", c=BT), X, ALU.add).then_inc(masks_done, 1)
            V.tensor_reduce(mask_t[:], ident[:].rearrange("p (t c) -> p t c", c=BT), X, ALU.add).then_inc(masks_done, 1)
            V.memset(ones_r[:].bitcast(f32), 1.0).then_inc(ones_done, 1)
            V.memset(pick_rs0[:].bitcast(f32), 0.0).then_inc(picks_zeroed, 1)
            V.memset(pick_bias[:], 0.0).then_inc(picks_zeroed, 1)
            V.memset(pick_rs1[:].bitcast(f32), 0.0).then_inc(picks_zeroed, 1)
            V.memset(sel[:], 0.0).then_inc(sel_zeroed, 1)
            dve.wait_ge(picks_zeroed, 3)
            V.memset(pick_rs0[:, 3 * L0N:3 * L0N + 3].bitcast(f32), 1.0).then_inc(picks_done, 1)
            V.memset(pick_bias[:, 3 * L0N + 3:K0], 1.0).then_inc(picks_done, 1)
            V.memset(pick_rs1[:, HB:K1].bitcast(f32), 1.0).then_inc(picks_done, 1)
            dve.wait_ge(ld_act, 16)
            dve.wait_ge(iotas_done, 3)
            V.tensor_scalar(act8[:], act_sb[:], float(R), None, ALU.mult).then_inc(act8_done, 1)
            V.tensor_copy(iota_e[:], iota_e_i[:]).then_inc(iota_e_done, 1)
            V.tensor_tensor(sel_r[:], iota_row[:], act_sb[0:E0, :], ALU.is_equal).then_inc(sel_r_done, 1)
            dve.wait_ge(act8_done, 1)
            dve.wait_ge(sel_zeroed, 1)
            for n in range(3):
                V.tensor_tensor(sel[:, n * L0N:(n + 1) * L0N].rearrange("p (s r) -> p s r", r=R), iota_slot[:],
                                act8[:].unsqueeze(2).to_broadcast([P, ACT0, R]), ALU.is_equal).then_inc(sel_done, 1)
            dve.wait_ge(ld_rt, 16)
            V.tensor_scalar(vcol2[:], rt_sb[:, D + 1:D + 2], EPS, None, ALU.add).then_inc(eps_done, 1)
            dve.wait_ge(am_mm, 1)
            V.tensor_tensor(am[:], p_z0[:, 0:MK], pack_sb[:, C_B2:C_B2 + MK], ALU.add).then_inc(am_done, 1)
            dve.wait_ge(am_done, 1)
            V.tensor_reduce(am_max[:], am[:], X, ALU.max, negate=True).then_inc(am_max_done, 1)
            dve.wait_ge(beta1_mm, 1)
            V.tensor_scalar(beta1[:], p_g0[:, 0:NT], pack_sb[:, C_FS:C_FS + 1], None, ALU.add).then_inc(beta1_done, BT)
            dve.wait_ge(am_exp_done, 1)
            V.reciprocal(am_rec[:], am_sum[:]).then_inc(am_rec_done, 1)
            dve.wait_ge(am_rec_done, 1)
            V.tensor_scalar(att[:], am_exp[:], am_rec[:], None, ALU.mult).then_inc(att_done, 1)
            dve.wait_ge(att_done, 1)
            dve.wait_ge(masks_done, 2)
            V.tensor_tensor(att_m[:], att[:].unsqueeze(1).to_broadcast([P, BT, MK]),
                            mask_c[:].unsqueeze(2).to_broadcast([P, BT, MK]), ALU.mult).then_inc(att_m_done, 1)
            dve.wait_ge(att_t_mm, 1)
            V.tensor_copy(att_t[:], p_z0[0:BT * MK, 0:NT]).then_inc(att_t_done, 1)
            dve.wait_ge(a0_hi_done, 1)
            V.tensor_tensor(a0_lo[:], p_h1[:, 0:HC * Z0N].rearrange("p (c n) -> p c n", c=HC), a0_hi[:].bitcast(f32),
                            ALU.subtract).then_inc(a0_lo_done, 1)
            dve.wait_ge(w_hi_done, 1)
            V.tensor_tensor(w_lo[:, 0], w_sb[:, 0], w_hi[:, 0].bitcast(f32), ALU.subtract).then_inc(w_lo_done, 1)
            dve.wait_ge(beta0_mm, 1)
            V.tensor_copy(beta0[:], p_g0[:, 0:NT]).then_inc(beta0_done, 1)
            n = 0
            for b in range(BT):
                for h, bank in enumerate((p_c1, p_y1)):
                    n += 1
                    dve.wait_ge(mix_hi_done, n)
                    rows = slice(b * CH, (b + 1) * CH)
                    cols = slice(b * CH + 16 * h, b * CH + 16 * h + 16)
                    V.tensor_tensor(mix_lo[rows, :, cols], bank[rows, :].rearrange("p (o t) -> p t o", t=NT),
                                    mix_hi[rows, :, cols].bitcast(f32), ALU.subtract).then_inc(mix_lo_done, 1)
            V.memset(beta5[:, :, 3:5], 1.0).then_inc(beta5_ones, 1)
            dve.wait_ge(beta0_done, 1)
            V.tensor_copy(beta5[:, :, 0].bitcast(f32r), beta0[:]).then_inc(beta5_hi, 1)
            dve.wait_ge(beta5_hi, 1)
            V.tensor_tensor(beta5[:, :, 1], beta0[:], beta5[:, :, 0], ALU.subtract).then_inc(beta5_lo, 1)
            dve.wait_ge(beta5_lo, 1)
            dve.wait_ge(beta5_ones, 1)
            V.tensor_copy(beta5[:, :, 2], beta5[:, :, 0]).then_inc(beta5_done, 1)
            dve.wait_ge(vlog_done, 1)
            V.tensor_tensor(vmat[:, 0:1], vcol[:], rt_sb[:, D:D + 1], ALU.add).then_inc(vcol2_done, 1)
            dve.wait_ge(vcol2_done, 1)
            V.tensor_copy(vmat[:, 1:P], vmat[:, 0:1].to_broadcast([E0, P - 1])).then_inc(vmat_done, 1)
            dve.wait_ge(rs0_mm, 1)
            V.tensor_copy(rs0[:], p_g1[:, 0:Z0N]).then_inc(rs0_done, 1)
            dve.wait_ge(vrow_mm, 1)
            V.tensor_copy(vrow[:], p_g1[:, 64:64 + ACT0]).then_inc(vrow_done, 1)
            dve.wait_ge(rs0_done, 1)
            V.tensor_tensor(z_add[:], rs0[:].unsqueeze(1).to_broadcast([P, NT, Z0N]),
                            beta0[:].unsqueeze(2).to_broadcast([P, NT, Z0N]), ALU.mult).then_inc(z_mul_done, 1)
            dve.wait_ge(z_mul_done, 1)
            dve.wait_ge(vrow_done, 1)
            V.tensor_tensor(z_add[:, :, L0N:Z0N], z_add[:, :, L0N:Z0N],
                            vrow[:].unsqueeze(1).to_broadcast([P, NT, ACT0]), ALU.add).then_inc(z_add_done, 1)
            dve.wait_ge(b0_round_done, 1)
            dve.wait_ge(lomask_done, 1)
            V.scalar_tensor_tensor(b0_stack[:], b0_round[:].bitcast(f32), minus_lo_row[0:K0], p_y0[0:K0, :],
                                   ALU.mult, ALU.add).then_inc(b0_done, 1)

            def step(s):
                if s.live():
                    after(dve, z0_mm, s)
                    if s.i is None and s.c == 0:
                        dve.wait_ge(z_add_done, 1)
                    V.tensor_tensor(z0[:], p_z0[:, 0:Z0N], z_add[:, s.n(), :], ALU.add).then_inc(z0_done, 1)
                    after(dve, z0_done, s)
                    V.tensor_reduce(z0_nmax[:], z0[:, L0N:Z0N], X, ALU.max, negate=True).then_inc(z0_nmax_done, 1)
                    after(dve, z0_exp_done, s)
                    V.reciprocal(z0_rec[:], z0_sum[:]).then_inc(z0_rec_done, 1)
                    after(dve, z0_rec_done, s)
                    V.tensor_scalar(alpha[:], z0_exp[:], z0_rec[:], SCALING, ALU.mult, ALU.mult).then_inc(alpha_done, 1)
                    after(dve, alpha_done, s)
                    V.tensor_tensor(g0[:].rearrange("p (s r) -> p s r", r=R), z0[:, 0:L0N].rearrange("p (s r) -> p s r", r=R),
                                    alpha[:].unsqueeze(2).to_broadcast([P, ACT0, R]), ALU.mult).then_inc(g0_done, 1)
                    after(dve, g0_done, s)
                    after(dve, g0_tr, s, -1)
                    V.tensor_copy(g0s[:, 0:3 * L0N].rearrange("p (a n) -> p a n", n=L0N)[:, 0:3:2, :].bitcast(f32r),
                                  g0[:].unsqueeze(1).to_broadcast([P, 2, L0N])).then_inc(g0_hi_done, 1)
                    after(dve, g0_hi_done, s)
                    V.tensor_tensor(g0s[:, L0N:2 * L0N], g0[:], g0s[:, 0:L0N], ALU.subtract).then_inc(g0_lo_done, 1)
                if (s + -3).live():
                    after(dve, g1t_hi_done, s, -3)
                    V.tensor_tensor(g1t_lo[:], p_g1[0:K1, 0:2 * P].rearrange("p (a n) -> p a n", a=2),
                                    g1t_hi[:].bitcast(f32), ALU.subtract).then_inc(g1t_lo_done, 1)
                if (s + -LAG).live():
                    after(dve, c1_hi_done, s, -LAG)
                    V.tensor_tensor(c1_lo[:].rearrange("p r (a o) -> p a r o", o=GC),
                                    p_c1[:].rearrange("p (a r o) -> p a r o", r=NPH, o=GC),
                                    c1_hi[:].bitcast(f32).rearrange("p r (a o) -> p a r o", o=GC),
                                    ALU.subtract).then_inc(c1_lo_done, 1)
                if (s + 1).live():
                    after(dve, c0_hi_done, s, 1)
                    V.tensor_tensor(c0_lo[:], p_c0[:], c0_hi[:].bitcast(f32), ALU.subtract).then_inc(c0_lo_done, 1)
                if (s + -3).live():
                    v = s + -3
                    after(dve, y1_mm, v)
                    after_dma(dve, y_stored, v, -2)
                    V.tensor_tensor(y_sb[:, v.mod(2), :].rearrange("p (q f) -> p f q", f=NPH),
                                    p_y1[:].rearrange("p (f q) -> p f q", f=NPH), x1[:, v.mod(4), :, 1:1 + NQ],
                                    ALU.add).then_inc(y_done, 1)
                if s.live():
                    after(dve, y0_mm, s)
                    after_dma(dve, x1_stored, s, -4)
                    V.tensor_tensor(x1[:, s.mod(4), :, 1:1 + NQ], p_y0[:].rearrange("p (f q) -> p f q", f=NPH),
                                    x_sb[:, s.mod(4), :].rearrange("p (q f) -> p f q", f=NPH), ALU.add).then_inc(x1_done, 1)
                if s.i is None and s.c == 0:
                    dve.wait_ge(a1_hi_done, 1)
                    V.tensor_tensor(a1_lo[:], a1_sb[:], a1_hi[:].bitcast(f32), ALU.subtract).then_inc(a1_lo_done, 1)
                    dve.wait_ge(w_hi_done, 2)
                    V.tensor_tensor(w_lo[:, 1], w_sb[:, 1], w_hi[:, 1].bitcast(f32), ALU.subtract).then_inc(w_lo_done, 1)
                if s.i is None and s.c == 1:
                    for a in range(2):
                        dve.wait_ge(b1_hi_done, a + 1)
                        V.tensor_tensor(b1_lo[:, a, :], (p_g1, p_h1)[a][0:K1, :], b1_hi[:, a, :].bitcast(f32),
                                        ALU.subtract).then_inc(b1_lo_done, 1)
                    dve.wait_ge(rs1_mm, 1)
                    V.tensor_copy(rs1[:], p_y1[:, 0:H1N]).then_inc(rs1_done, 1)
                if (s + -LAG).live():
                    v = s + -LAG
                    after(dve, h1_mm, v)
                    if v.i is None and v.c == 0:
                        dve.wait_ge(rs1_done, 1)
                        dve.wait_ge(beta1_done, BT)
                        dve.wait_ge(iota_e_done, 1)
                    beta = beta1[:, bass.ds(v.n(), 1)]
                    V.scalar_tensor_tensor(h1[:, L1N:H1N], rs1[:, L1N:H1N], beta, p_h1[:, L1N:H1N],
                                           ALU.mult, ALU.add).then_inc(logits_done, 1)
                    after(dve, logits_done, v)
                    V.scalar_tensor_tensor(h1[:, 0:L1N], rs1[:, 0:L1N], beta, p_h1[:, 0:L1N],
                                           ALU.mult, ALU.add).then_inc(h1_done, 1)
                    V.max(top[:], h1[:, L1N:H1N]).then_inc(top_done, 1)
                    after(dve, top_done, v)
                    V.tensor_scalar(ntop[:], top[:, 0:1], -1.0, None, ALU.mult).then_inc(ntop_done, 1)
                    V.max_index(top_i[:], top[:], h1[:, L1N:H1N]).then_inc(top_i_done, 1)
                    after(dve, top_i_done, v)
                    V.tensor_copy(top_f[:], top_i[:, 0:2]).then_inc(top_f_done, 1)
                    after(dve, t_exp_done, v)
                    V.reciprocal(t_rec[:], t_sum[:]).then_inc(t_rec_done, 1)
                    after(dve, t_rec_done, v)
                    V.tensor_scalar(prob[:], t_exp[:], t_rec[:], SCALING, ALU.mult, ALU.mult).then_inc(prob_done, 1)
                    after(dve, prob_done, v)
                    after(dve, top_f_done, v)
                    V.tensor_scalar(gate_a[:], iota_e[:], top_f[:, 0:1], prob[:, 0:1], ALU.is_equal, ALU.mult).then_inc(gate_a_done, 1)
                    V.tensor_scalar(gate_b[:], iota_e[:], top_f[:, 1:2], prob[:, 1:2], ALU.is_equal, ALU.mult).then_inc(gate_b_done, 1)
                    after(dve, gate_a_done, v)
                    after(dve, gate_b_done, v)
                    V.tensor_tensor(gate[:], gate_a[:], gate_b[:], ALU.add).then_inc(gate_done, 1)
                    after(dve, gate_done, v)
                    after(dve, h1_done, v)
                    after(dve, g1_tr, v, -1)
                    V.tensor_tensor(g1[:, :, 0:HB].rearrange("p a (e r) -> p a e r", r=R),
                                    h1[:, 0:L1N].rearrange("p (a e r) -> p a e r", a=2, r=R),
                                    gate[:].rearrange("p (a e) -> p a e", a=2).unsqueeze(3).to_broadcast([P, 2, E1 // 2, R]),
                                    ALU.mult).then_inc(g1_done, 1)

            dve.wait_ge(x1_padded, 2)
            steps(dve, step, -1, NT + 2, 3, 7)

        @block.tensor
        def _(pe):
            mm = nc.tensor.matmul

            def split_mm(psum, lhs, rhs, start, stop):
                mm(psum, lhs[0], rhs[0], start=start, stop=False)
                mm(psum, lhs[0], rhs[1], start=False, stop=False)
                return mm(psum, lhs[1], rhs[0], start=False, stop=stop)

            pe.wait_ge(ld_pack, 16)
            cond = pack_sb[:, C_COND:C_COND + BATCH]
            mm(p_c0[:, 0:P], pack_sb[:, C_W0:C_W0 + P], cond, start=True, stop=True).then_inc(u1_mm, 1)
            for b in range(BT):
                last = mm(p_g0[b * CH:(b + 1) * CH, 0:NT], pack_sb[:, C_CW:C_CW + CH],
                          cond.rearrange("p (t b) -> p b t", b=BT)[:, b, :], start=True, stop=True)
            last.then_inc(beta1_mm, 1)
            pe.wait_ge(m1_done, 1)
            mm(p_c0[:, 0:P], pack_sb[:, C_W1:C_W1 + P], m1[:], start=True, stop=True).then_inc(u2_mm, 1)
            pe.wait_ge(m2_done, 1)
            mm(p_z0[:, 0:MK], m2[:], pack_sb[:, C_W2:C_W2 + MK], start=True, stop=True).then_inc(am_mm, 1)
            pe.wait_ge(sel_done, 3)
            pe.wait_ge(sel_r_done, 1)
            pe.wait_ge(ld_exp, 16)
            pe.wait_ge(ld_rt, 16)
            for c in range(HC):
                mm(p_h1[:, c * Z0N:c * Z0N + L0N], exp_sb[:, 0, c * P:(c + 1) * P], sel[:, 0:L0N], start=True, stop=True)
                last = mm(p_h1[:, c * Z0N + L0N:(c + 1) * Z0N], rt_sb[:, c * P:(c + 1) * P], sel_r[:], start=True, stop=True)
            last.then_inc(a0_mm, 1)
            pe.wait_ge(att_m_done, 1)
            mm(p_z0[0:BT * MK, 0:NT], att_m[:].rearrange("p b k -> p (b k)"), mask_t[:], start=True, stop=True).then_inc(att_t_mm, 1)
            pe.wait_ge(att_t_done, 1)
            pe.wait_ge(ld_kw, 16)
            for o in range(CH):
                bank = (p_c1, p_y1)[o // 16]
                last = mm(bank[:, (o % 16) * NT:(o % 16 + 1) * NT], kw_sb[:, o, :], att_t[:], start=True, stop=True)
            last.then_inc(mix_mm, 1)
            pe.wait_ge(beta1_done, BT)
            mm(p_g0[:, 0:NT], kw_sb[:, CH, :], att_t[:], start=True, stop=True).then_inc(beta0_mm, 1)
            pe.wait_ge(a0_lo_done, 1)
            pe.wait_ge(ones_done, 1)
            for c in range(HC):
                for h, half in enumerate((a0_hi, a0_lo)):
                    last = mm(p_g1[:, 0:Z0N], ones_r[:], half[:, c, :], start=(c + h == 0), stop=(c == HC - 1 and h == 1))
            last.then_inc(rs0_mm, 1)
            pe.wait_ge(rs0_done, 1)
            pe.wait_ge(vmat_done, 1)
            mm(p_g1[:, 64:64 + ACT0], vmat[:], sel_r[:], start=True, stop=True).then_inc(vrow_mm, 1)
            pe.wait_ge(w_lo_done, 1)
            pe.wait_ge(picks_done, 3)
            pe.wait_ge(ld_bb, 16)
            mm(p_y0[0:K0, :], sel[:], exp_sb[:, 1, :], start=True, stop=False)
            for c in range(HC):
                mm(p_y0[0:K0, :], pick_rs0[:], w_hi[:, 0, c, :], start=False, stop=False)
                mm(p_y0[0:K0, :], pick_rs0[:], w_lo[:, 0, c, :], start=False, stop=False)
            mm(p_y0[0:K0, :], pick_bias[:], bb_sb[:], start=False, stop=True).then_inc(b0_mm, 1)
            pe.wait_ge(mix_lo_done, 2 * BT)

            def step(s):
                if s.live():
                    after(pe, c0_lo_done, s)
                    after(pe, z0_done, s, -1)
                    for c in range(HC):
                        cols = slice(c * P, (c + 1) * P)
                        last = split_mm(p_z0[:, 0:Z0N], (c0_hi[:, cols], c0_lo[:, cols]), (a0_hi[:, c, :], a0_lo[:, c, :]),
                                        c == 0, c == HC - 1)
                    last.then_inc(z0_mm, 1)
                    if s.i is None and s.c == 0:
                        pe.wait_ge(b0_done, 1)
                    after(pe, x1_done, s, -1)
                    for c in range(HC):
                        cols = slice(c * P, (c + 1) * P)
                        split_mm(p_y0[:], (c0_hi[:, cols], c0_lo[:, cols]), (w_hi[:, 0, c, :], w_lo[:, 0, c, :]), c == 0, False)
                if (s + -3).live():
                    v = s + -3
                    after(pe, g1_done, v)
                    after(pe, g1_beta_done, v)
                    after(pe, g1t_lo_done, v, -1)
                    if v.i is None and v.c == 0:
                        pe.wait_ge(g1_padded, 1)
                        pe.wait_ge(b1_lo_done, 2)
                    for a in range(2):
                        last = nc.tensor.transpose(p_g1[0:K1, a * P:(a + 1) * P], g1[:, a, :], ident[:])
                    last.then_inc(g1_tr, 1)
                if (s + -LAG).live():
                    v = s + -LAG
                    after_dma(pe, win_loaded, v, 0, 16 * WIN)
                    after(pe, c1_lo_done, v, -1)
                    if v.i is None and v.c == 0:
                        pe.wait_ge(ld_wc, 16)
                    for a in range(CG):
                        last = mm(p_c1[:, a * CH:(a + 1) * CH], win[:, v.mod(2), a, :], wc_sb[:, a % GROUPS, :],
                                  start=True, stop=True)
                    last.then_inc(c1_mm, 1)
                if s.live():
                    after(pe, g0_lo_done, s)
                    after(pe, g0_beta_done, s)
                    after(pe, g0t_done, s, -1)
                    nc.tensor.transpose(p_g0[0:K0, 0:P], g0s[:], ident[:]).then_inc(g0_tr, 1)
                if (s + 1).live():
                    t = s + 1
                    after(pe, x_lo_done, t)
                    after(pe, c0_lo_done, s)
                    for c in range(HC):
                        cols = slice(c * P, (c + 1) * P)
                        last = split_mm(p_c0[:, cols], (x_hi[:, t.mod(2), cols], x_lo[:, t.mod(2), cols]),
                                        (mix_hi[:, t.n(), :], mix_lo[:, t.n(), :]), True, True)
                    last.then_inc(c0_mm, 1)
                if (s + -3).live():
                    after(pe, g1t_lo_done, s, -3)
                    for a in range(2):
                        last = split_mm(p_y1[:], (g1t_hi[:, a, :], g1t_lo[:, a, :]), (b1_hi[:, a, :], b1_lo[:, a, :]),
                                        False, a == 1)
                    last.then_inc(y1_mm, 1)
                if s.live():
                    after(pe, g0t_done, s)
                    mm(p_y0[:], g0t[:], b0_stack[:], start=False, stop=True).then_inc(y0_mm, 1)
                if s.i is None and s.c == 0:
                    pe.wait_ge(ld_b1, 16)
                    mm(p_g1[0:K1, :], ident[0:HB, 0:K1], b1_sb[:, 0, :], start=True, stop=True).then_inc(b1_mm, 1)
                    mm(p_h1[0:K1, :], ident[0:HB, 0:K1], b1_sb[:, 1, :], start=True, stop=False)
                    pe.wait_ge(w_lo_done, 2)
                    for c in range(HC):
                        mm(p_h1[0:K1, :], pick_rs1[:], w_hi[:, 1, c, :], start=False, stop=False)
                        last = mm(p_h1[0:K1, :], pick_rs1[:], w_lo[:, 1, c, :], start=False, stop=(c == HC - 1))
                    last.then_inc(b1_mm, 1)
                    for c in range(HC):
                        mm(p_y1[:, 0:H1N], ones_r[:], a1_hi[:, c, :], start=(c == 0), stop=False)
                        last = mm(p_y1[:, 0:H1N], ones_r[:], a1_lo[:, c, :], start=False, stop=(c == HC - 1))
                    last.then_inc(rs1_mm, 1)
                if (s + -LAG).live():
                    v = s + -LAG
                    after(pe, c1_lo_done, v)
                    after(pe, h1_done, v, -1)
                    if v.i is None and v.c == 0:
                        pe.wait_ge(b1_lo_done, 2)
                        pe.wait_ge(rs1_done, 1)
                    for c in range(HC):
                        last = split_mm(p_h1[:, 0:H1N], (c1_hi[:, c, :], c1_lo[:, c, :]), (a1_hi[:, c, :], a1_lo[:, c, :]),
                                        c == 0, c == HC - 1)
                    last.then_inc(h1_mm, 1)
                    after(pe, y_done, v, -1)
                    for c in range(HC):
                        split_mm(p_y1[:], (c1_hi[:, c, :], c1_lo[:, c, :]), (w_hi[:, 1, c, :], w_lo[:, 1, c, :]), c == 0, False)

            steps(pe, step, -1, NT + 2, 3, 7)


def by_phase(a):
    return np.ascontiguousarray(a.reshape(*a.shape[:-1], NQ, NPH).swapaxes(-1, -2)).reshape(a.shape)


def lay_out(i):
    f = np.float32
    pack = np.zeros((P, C_END), f)
    pack[:, C_COND:C_COND + BATCH] = i["cond_128"].T
    pack[:, C_W0:C_W0 + P] = i["L0_cond_W0"]
    pack[:, C_W1:C_W1 + P] = i["L0_cond_W1"]
    pack[:, C_W2:C_W2 + MK] = i["L0_cond_W2"]
    pack[:, C_B2:C_B2 + MK] = i["L0_cond_b2"][None, :]
    pack[:, C_B0] = i["L0_cond_b0"]
    pack[:, C_B1] = i["L0_cond_b1"]
    pack[:, C_FS] = np.tile(i["fside_S_0"], BT)
    pack[:, C_CW:C_CW + CH] = i["L1_cond_c_weight"].T
    kw = np.zeros((BT, MK, CH + 1, BT, CH), f)
    for b in range(BT):
        kw[b, :, :CH, b, :] = i["L0_cond_weight"][..., 0]
        kw[b, :, CH, b, :] = i["L0_cond_bias_k"]
    experts = np.stack([i["L0_ffn_lora_A"].reshape(P, D),
                        by_phase(i["L0_ffn_lora_B"].transpose(0, 2, 1).reshape(P, D))], 1)
    router = np.concatenate([i["L0_ffn_router_W"], i["L0_ffn_router_b"][:, None], i["L0_ffn_domain_prior"][:, None]], 1)
    w0 = by_phase(i["L0_ffn_W_base"].T).reshape(HC, P, D).transpose(1, 0, 2)
    w1 = by_phase(i["L1_ffn_base_W"].T).reshape(NQ, NPH * D)
    a1 = np.concatenate([i["L1_ffn_lora_A"].reshape(L1N, D), i["L1_ffn_gate_W"]], 0).T.reshape(NQ, NPH * H1N)
    b1 = by_phase(i["L1_ffn_lora_B"].transpose(0, 2, 1).reshape(L1N, D)).reshape(2, HB, D).transpose(1, 0, 2)
    wc = np.zeros((WIN, GC, GROUPS, NPH, GC), f)
    w = i["L1_cond_weight"].reshape(GROUPS, GC, GC, TAPS)
    for s in range(WIN):
        for r in range(NPH):
            if 0 <= s - r < TAPS:
                wc[s, :, :, r, :] = w[:, :, :, s - r].transpose(2, 0, 1)
    c = np.ascontiguousarray
    return {
        "x": c(i["x"]), "pack": pack, "kw": c(kw.reshape(BT * MK, -1)), "experts": c(experts.reshape(P, -1)),
        "router": c(router), "active": c(np.broadcast_to(i["L0_ffn_active"], (P, ACT0))),
        "b_base": c(by_phase(i["L0_ffn_b_base"])[None, :]), "w0": c(w0.reshape(P, -1)), "w1": c(w1), "a1": c(a1),
        "b1": c(b1.reshape(HB, -1)), "wc": c(wc.reshape(KIM, -1)),
    }


def kernel(**inputs):
    import concourse.bacc as bacc
    from concourse.bass_utils import run_bass_kernel_spmd

    arrays = lay_out({k: np.asarray(v) for k, v in inputs.items()})
    nc = bacc.Bacc("TRN2", target_bir_lowering=False, num_devices=1)
    args = {n: nc.dram_tensor(f"in_{n}", a.shape, mybir.dt.from_np(a.dtype), kind="ExternalInput").ap()
            for n, a in arrays.items()}
    out = nc.dram_tensor("out", (BATCH, CH, D), mybir.dt.float32, kind="ExternalOutput").ap()
    build(nc, out=out, **args)
    r = run_bass_kernel_spmd(nc, [{f"in_{n}": a for n, a in arrays.items()}], core_ids=[0])
    return r.results[0]["out"]
```

```python
import numpy as np

import concourse.bass as bass
from concourse import mybir
from contextlib import ExitStack

P = 128
BATCH, CH, D = 128, 32, 512
BT = P // CH
NT = BATCH // BT
HC = D // P
NPH, NQ = 4, D // 4
GROUPS, GC, TAPS = 4, 8, 9
CG = BT * GROUPS
WIN = 12
KIM = WIN * GC
NQP = NQ + 2
E0, ACT0, R = 16, 4, 8
L0N = ACT0 * R
Z0N = L0N + ACT0
E1 = 28
L1N = E1 * R
H1N = L1N + E1
HB = L1N // 2
K1 = HB + 1
K0 = 3 * L0N + 5
MK = 8
SCALING = 2.0
EPS = 1e-12
UNROLL, LAG = 4, 2

C_COND, C_W0, C_W1, C_W2, C_B2, C_B0, C_B1, C_FS, C_CW = 0, 128, 256, 384, 392, 400, 401, 402, 403
C_END = C_CW + CH


class Tile:

    def __init__(self, i, c):
        self.i, self.c = i, c

    def __add__(self, n):
        return Tile(self.i, self.c + n)

    def n(self):
        return self.c if self.i is None else self.i * UNROLL + self.c

    def mod(self, m):
        return self.c % m

    def over(self, m):
        return self.c // m if self.i is None else self.i * (UNROLL // m) + self.c // m

    def live(self):
        return self.i is not None or 0 <= self.c < NT


def steps(engine, step, first, last, loop_from, loops):
    for c in range(first, loop_from):
        step(Tile(None, c))
    with engine.Fori(0, loops) as i:
        for u in range(UNROLL):
            step(Tile(i, loop_from + u))
    for c in range(loop_from + loops * UNROLL, last + 1):
        step(Tile(None, c))


def build(nc, x, pack, kw, experts, router, active, b_base, w0, w1, a1, b1, wc, out):
    f32, f32r, i32, u32 = mybir.dt.float32, mybir.dt.float32r, mybir.dt.int32, mybir.dt.uint32
    ALU = mybir.AluOpType
    ACT = mybir.ActivationFunctionType
    X = mybir.AxisListType.X

    ctx = ExitStack()
    with ctx:
        def sb(name, shape, dt=f32):
            return ctx.enter_context(nc.sbuf_tensor(name, shape, dt))

        def pb(name):
            return ctx.enter_context(nc.psum_tensor(name, [P, 512], f32))

        def sem(name):
            return ctx.enter_context(nc.semaphore(name))

        scratch = nc.dram_tensor("x1_scratch", (NT, P, NPH, NQP), f32, kind="Internal").ap()

        pack_sb = sb("pack_sb", [P, C_END])
        kw_sb = sb("kw_sb", [BT * MK, CH + 1, P])
        exp_sb = sb("exp_sb", [P, 2, D])
        rt_sb = sb("rt_sb", [E0, D + 2])
        act_sb = sb("act_sb", [P, ACT0], i32)
        bb_sb = sb("bb_sb", [1, D])
        w0_sb = sb("w0_sb", [P, HC, D])
        w1_sb = sb("w1_sb", [P, HC, D])
        a1_sb = sb("a1_sb", [P, HC, H1N])
        b1_sb = sb("b1_sb", [HB, 2, D])
        wc_sb = sb("wc_sb", [KIM, GROUPS, NPH * GC])
        w0_hi = sb("w0_hi", [P, HC, Z0N + D], f32r)
        w0_lo = sb("w0_lo", [P, HC, Z0N + D], f32r)
        w1_hi = sb("w1_hi", [P, HC, D], f32r)
        w1_lo = sb("w1_lo", [P, HC, D], f32r)
        a1_hi = sb("a1_hi", [P, HC, H1N], f32r)
        a1_lo = sb("a1_lo", [P, HC, H1N], f32r)
        b0_round = sb("b0_round", [K0, D], f32r)
        b0_stack = sb("b0_stack", [K0, D], f32r)
        b1_hi = sb("b1_hi", [K1, 2, D], f32r)
        b1_lo = sb("b1_lo", [K1, 2, D], f32r)
        mix = sb("mix", [P, NT, P])

        ident = sb("ident", [P, P])
        ones_r = sb("ones_r", [P, P], f32r)
        pick_rs0 = sb("pick_rs0", [P, K0], f32r)
        pick_bias = sb("pick_bias", [1, K0])
        pick_rs1 = sb("pick_rs1", [P, K1], f32r)
        minus_lo_row = sb("minus_lo_row", [P, 1])
        iota_slot = sb("iota_slot", [P, ACT0, R], i32)
        iota_row = sb("iota_row", [E0, ACT0], i32)
        iota_e_i = sb("iota_e_i", [P, E1], i32)
        iota_e = sb("iota_e", [P, E1])
        act8 = sb("act8", [P, ACT0])
        sel = sb("sel", [P, K0])
        sel_r = sb("sel_r", [E0, ACT0])
        mask_c = sb("mask_c", [P, BT])
        mask_t = sb("mask_t", [P, NT])

        m1 = sb("m1", [P, BATCH])
        m2 = sb("m2", [P, BATCH])
        am = sb("am", [P, MK])
        am_max = sb("am_max", [P, 1])
        am_exp = sb("am_exp", [P, MK])
        am_sum = sb("am_sum", [P, 1])
        am_rec = sb("am_rec", [P, 1])
        att = sb("att", [P, MK])
        att_m = sb("att_m", [P, BT, MK])
        att_t = sb("att_t", [BT * MK, NT])
        beta0 = sb("beta0", [P, NT])
        beta1 = sb("beta1", [P, NT])
        beta5 = sb("beta5", [P, NT, 5])
        rs0 = sb("rs0", [P, Z0N])
        vcol = sb("vcol", [E0, 1])
        vcol2 = sb("vcol2", [E0, 1])
        vmat = sb("vmat", [E0, P])
        vrow = sb("vrow", [P, ACT0])
        z_add = sb("z_add", [P, NT, Z0N])
        rs1 = sb("rs1", [P, H1N])

        x_sb = sb("x_sb", [P, 4, D])
        c0_hi = sb("c0_hi", [P, 2, D], f32r)
        c0_lo = sb("c0_lo", [P, 2, D], f32r)
        z0 = sb("z0", [P, Z0N])
        z0_nmax = sb("z0_nmax", [P, 1])
        z0_exp = sb("z0_exp", [P, ACT0])
        z0_sum = sb("z0_sum", [P, 1])
        z0_rec = sb("z0_rec", [P, 1])
        alpha = sb("alpha", [P, ACT0])
        g0 = sb("g0", [P, L0N])
        g0s = sb("g0s", [P, K0])
        g0t = sb("g0t", [K0, P], f32r)
        x1 = sb("x1", [P, 4, NPH, NQP])
        win = sb("win", [KIM, 2, CG, NQ])
        cv = sb("cv", [P, D])
        c1_hi = sb("c1_hi", [P, NPH, P], f32r)
        c1_lo = sb("c1_lo", [P, NPH, P], f32r)
        h1 = sb("h1", [P, H1N])
        top = sb("top", [P, 8])
        top_i = sb("top_i", [P, 8], u32)
        top_f = sb("top_f", [P, 2])
        ntop = sb("ntop", [P, 1])
        t_exp = sb("t_exp", [P, 2])
        t_sum = sb("t_sum", [P, 1])
        t_rec = sb("t_rec", [P, 1])
        prob = sb("prob", [P, 2])
        gate_a = sb("gate_a", [P, E1])
        gate_b = sb("gate_b", [P, E1])
        gate = sb("gate", [P, E1])
        g1 = sb("g1", [P, 2, K1])
        g1t_hi = sb("g1t_hi", [K1, 2, P], f32r)
        g1t_lo = sb("g1t_lo", [K1, 2, P], f32r)
        y_sb = sb("y_sb", [P, 2, D])

        p_c0, p_y0a, p_y0b, p_g = pb("p_c0"), pb("p_y0a"), pb("p_y0b"), pb("p_g")
        p_cv, p_c1, p_h1, p_y1 = pb("p_cv"), pb("p_c1"), pb("p_h1"), pb("p_y1")
        p_g1t = p_g[0:K1, 0:2 * P].rearrange("p (a n) -> p a n", a=2)
        p_g0t = p_g[0:K0, 2 * P:3 * P]
        NY = D // 2
        p_y0 = (p_y0a[:, Z0N:Z0N + NY], p_y0b[:, 0:NY])

        ld_pack, ld_kw, ld_exp, ld_rt = sem("ld_pack"), sem("ld_kw"), sem("ld_exp"), sem("ld_rt")
        ld_act, ld_bb, ld_w0, ld_w1 = sem("ld_act"), sem("ld_bb"), sem("ld_w0"), sem("ld_w1")
        ld_a1, ld_b1, ld_wc = sem("ld_a1"), sem("ld_b1"), sem("ld_wc")
        x_loaded = [sem(f"x_loaded{n}") for n in range(4)]
        x1_stored = [sem(f"x1_stored{n}") for n in range(4)]
        win_loaded = [sem(f"win_loaded{n}") for n in range(2)]
        y_stored = [sem(f"y_stored{n}") for n in range(2)]

        zeroed_id, ident_done, ones_done, picks_zeroed = sem("zeroed_id"), sem("ident_done"), sem("ones_done"), sem("picks_zeroed")
        picks_done, iotas_done, mix_zeroed, x1_padded = sem("picks_done"), sem("iotas_done"), sem("mix_zeroed"), sem("x1_padded")
        g1_padded, lomask_0, lomask_1, lomask_2, lomask_done = sem("g1_padded"), sem("lomask_0"), sem("lomask_1"), sem("lomask_2"), sem("lomask_done")
        masks_done, u1_mm, m1_done = sem("masks_done"), sem("u1_mm"), sem("m1_done")
        u2_mm, m2_done = sem("u2_mm"), sem("m2_done")
        am_mm, am_done, am_max_done, am_exp_done = sem("am_mm"), sem("am_done"), sem("am_max_done"), sem("am_exp_done")
        am_rec_done, att_done, att_m_done, att_t_mm, att_t_done = sem("am_rec_done"), sem("att_done"), sem("att_m_done"), sem("att_t_mm"), sem("att_t_done")
        beta1_mm, beta1_done, beta0_mm, beta0_done = sem("beta1_mm"), sem("beta1_done"), sem("beta0_mm"), sem("beta0_done")
        mix_mm, mix_a_done, mix_b_done = sem("mix_mm"), sem("mix_a_done"), sem("mix_b_done")
        iota_e_done, act8_done, sel_zeroed, sel_done, sel_r_done = sem("iota_e_done"), sem("act8_done"), sem("sel_zeroed"), sem("sel_done"), sem("sel_r_done")
        a0_mm, a0_hi_done, a0_lo_done = sem("a0_mm"), sem("a0_hi_done"), sem("a0_lo_done")
        w0_hi_done, w0_lo_done = sem("w0_hi_done"), sem("w0_lo_done")
        w1_hi_done, w1_lo_done = sem("w1_hi_done"), sem("w1_lo_done")
        a1_hi_done, a1_lo_done = sem("a1_hi_done"), sem("a1_lo_done")
        b0_mm, b0_round_done, b0_done = sem("b0_mm"), sem("b0_round_done"), sem("b0_done")
        b1_mm, b1_hi_done, b1_lo_done = sem("b1_mm"), sem("b1_hi_done"), sem("b1_lo_done")
        rs0_mm, rs0_done, vlog_done, vcol2_done, vmat_done = sem("rs0_mm"), sem("rs0_done"), sem("vlog_done"), sem("vcol2_done"), sem("vmat_done")
        vrow_mm, vrow_done, z_mul_done, z_add_done = sem("vrow_mm"), sem("vrow_done"), sem("z_mul_done"), sem("z_add_done")
        rs1_mm, rs1_done = sem("rs1_mm"), sem("rs1_done")
        beta5_ones, beta5_hi, beta5_lo, beta5_done = sem("beta5_ones"), sem("beta5_hi"), sem("beta5_lo"), sem("beta5_done")
        eps_done = sem("eps_done")

        cv_mm, cv_done = sem("cv_mm"), sem("cv_done")
        c0_mm, c0_hi_done, c0_lo_done = sem("c0_mm"), sem("c0_hi_done"), sem("c0_lo_done")
        z0_mm, z0_done, z0_nmax_done, z0_exp_done = sem("z0_mm"), sem("z0_done"), sem("z0_nmax_done"), sem("z0_exp_done")
        z0_rec_done, alpha_done, g0_done, g0_hi_done = sem("z0_rec_done"), sem("alpha_done"), sem("g0_done"), sem("g0_hi_done")
        g0_lo_done, g0_beta_done = sem("g0_lo_done"), sem("g0_beta_done")
        g0_tr, g0t_done, y0_mm, x1_done = sem("g0_tr"), sem("g0t_done"), sem("y0_mm"), sem("x1_done")
        c1_tr, c1_hi_done, c1_lo_done = sem("c1_tr"), sem("c1_hi_done"), sem("c1_lo_done")
        h1_mm, logits_done, h1_done, top_done, top_i_done, ntop_done = sem("h1_mm"), sem("logits_done"), sem("h1_done"), sem("top_done"), sem("top_i_done"), sem("ntop_done")
        top_f_done, t_exp_done, t_rec_done, prob_done = sem("top_f_done"), sem("t_exp_done"), sem("t_rec_done"), sem("prob_done")
        gate_a_done, gate_b_done, gate_done, g1_done, g1_beta_done = sem("gate_a_done"), sem("gate_b_done"), sem("gate_done"), sem("g1_done"), sem("g1_beta_done")
        g1_tr, g1t_hi_done, g1t_lo_done = sem("g1_tr"), sem("g1t_hi_done"), sem("g1t_lo_done")
        y1_mm, y_done = sem("y1_mm"), sem("y_done")

        x_v = x.rearrange("(t b) c h -> t (b c) h", b=BT)
        out_v = out.rearrange("(t b) c h -> t (b c) h", b=BT)
        windows = scratch.rearrange("t (a i) f q -> t (i f) a q", i=GC)

        block = ctx.enter_context(nc.Block())

        def after(eng, semaphore, tile, ahead=0):
            t = tile + ahead
            if t.live():
                eng.wait_ge(semaphore, t.n() + 1)

        def after_dma(eng, semaphores, tile, ahead=0, count=16):
            t = tile + ahead
            if t.live():
                m = len(semaphores)
                eng.wait_ge(semaphores[t.mod(m)], (t.over(m) + 1) * count)

        @block.sync
        def _(sp):
            sp.dma_start(pack_sb[:], pack).then_inc(ld_pack, 16)
            sp.dma_start(act_sb[:], active).then_inc(ld_act, 16)
            sp.dma_start(kw_sb[:], kw.rearrange("k (o p) -> k o p", p=P)).then_inc(ld_kw, 16)
            sp.dma_start(x_sb[:, 0, :], x_v[0]).then_inc(x_loaded[0], 16)
            sp.dma_start(exp_sb[:], experts.rearrange("p (a d) -> p a d", a=2)).then_inc(ld_exp, 16)
            sp.dma_start(rt_sb[:], router).then_inc(ld_rt, 16)
            sp.dma_start(w0_sb[:], w0.rearrange("p (c d) -> p c d", c=HC)).then_inc(ld_w0, 16)
            sp.dma_start(bb_sb[:], b_base).then_inc(ld_bb, 16)
            sp.dma_start(x_sb[:, 1, :], x_v[1]).then_inc(x_loaded[1], 16)
            sp.dma_start(a1_sb[:], a1.rearrange("p (c n) -> p c n", c=HC)).then_inc(ld_a1, 16)
            sp.dma_start(w1_sb[:], w1.rearrange("p (c d) -> p c d", c=HC)).then_inc(ld_w1, 16)
            sp.dma_start(wc_sb[:], wc.rearrange("k (g n) -> k g n", g=GROUPS)).then_inc(ld_wc, 16)
            sp.dma_start(b1_sb[:], b1.rearrange("p (a d) -> p a d", a=2)).then_inc(ld_b1, 16)

            def step(s):
                if (s + -1).live():
                    v = s + -1
                    after_dma(sp, x1_stored, v)
                    after(sp, cv_mm, v, -2)
                    for j in range(WIN // NPH):
                        rows = slice(j * NPH * GC, (j + 1) * NPH * GC)
                        sp.dma_start(win[rows, v.mod(2)], windows[v.n()][:, :, j:j + NQ]).then_inc(win_loaded[v.mod(2)], 16)
                if (s + 2).live() and (s.i is not None or s.c >= 0):
                    after(sp, x1_done, s, -2)
                    sp.dma_start(x_sb[:, (s + 2).mod(4), :], x_v[(s + 2).n()]).then_inc(x_loaded[(s + 2).mod(4)], 16)
                if (s + -3).live():
                    v = s + -3
                    after(sp, y_done, v)
                    sp.dma_start(out_v[v.n()], y_sb[:, v.mod(2), :]).then_inc(y_stored[v.mod(2)], 16)
                if s.live():
                    after(sp, x1_done, s)
                    sp.dma_start(scratch[s.n()], x1[:, s.mod(4)]).then_inc(x1_stored[s.mod(4)], 16)

            steps(sp, step, 0, NT + 2, 3, 6)
            for n in range(2):
                sp.wait_ge(y_stored[n], 16 * NT // 2)

        @block.gpsimd
        def _(pool):
            pool.memset(ident[:], 0.0).then_inc(zeroed_id, 1)
            pool.wait_ge(zeroed_id, 1)
            pool.affine_select(out=ident[:], in_=ident[:], compare_op=ALU.not_equal, fill=1.0, base=0,
                               pattern=[[-1, P]], channel_multiplier=1).then_inc(ident_done, 1)
            pool.iota(iota_slot[:], pattern=[[0, ACT0], [-1, R]], base=0, channel_multiplier=1).then_inc(iotas_done, 1)
            pool.iota(iota_row[:], pattern=[[0, ACT0]], base=0, channel_multiplier=1).then_inc(iotas_done, 1)
            pool.iota(iota_e_i[:], pattern=[[1, E1]], base=0, channel_multiplier=0).then_inc(iotas_done, 1)
            pool.memset(minus_lo_row[:], 0.0).then_inc(lomask_0, 1)
            pool.wait_ge(lomask_0, 1)
            pool.memset(minus_lo_row[2 * L0N:3 * L0N], -1.0).then_inc(lomask_1, 1)
            pool.wait_ge(lomask_1, 1)
            pool.affine_select(out=minus_lo_row[:], in_=minus_lo_row[:], compare_op=ALU.not_equal, fill=-1.0,
                               base=-(3 * L0N + 2), pattern=[[0, 1]], channel_multiplier=1).then_inc(lomask_2, 1)
            pool.wait_ge(lomask_2, 1)
            pool.affine_select(out=minus_lo_row[:], in_=minus_lo_row[:], compare_op=ALU.not_equal, fill=-1.0,
                               base=-(3 * L0N + 4), pattern=[[0, 1]], channel_multiplier=1).then_inc(lomask_done, 1)
            pool.memset(mix[:], 0.0).then_inc(mix_zeroed, 1)
            pool.memset(g1[:, 0, HB:K1], 0.0).then_inc(g1_padded, 1)
            for f in range(2):
                pool.memset(x1[:, :, :, f * (NQP - 1):f * (NQP - 1) + 1], 0.0).then_inc(x1_padded, 1)

            def step(s):
                if s.live():
                    if s.i is None and s.c == 0:
                        pool.wait_ge(beta5_done, 1)
                    after(pool, g0_tr, s, -1)
                    pool.tensor_copy(g0s[:, 3 * L0N:K0], beta5[:, s.n(), :]).then_inc(g0_beta_done, 1)
                if (s + -LAG).live():
                    v = s + -LAG
                    if v.i is None and v.c == 0:
                        pool.wait_ge(beta1_done, BT)
                    after(pool, g1_tr, v, -1)
                    pool.tensor_copy(g1[:, 1, HB:K1], beta1[:, bass.ds(v.n(), 1)]).then_inc(g1_beta_done, 1)

            steps(pool, step, 0, NT + 1, 3, 7)

        @block.scalar
        def _(act):
            act.wait_ge(ld_pack, 16)
            act.wait_ge(u1_mm, 1)
            nc.scalar.activation(m1[:], p_c0[:, 0:P], ACT.Gelu, bias=pack_sb[:, C_B0:C_B0 + 1]).then_inc(m1_done, 1)
            act.wait_ge(u2_mm, 1)
            nc.scalar.activation(m2[:], p_c0[:, 0:P], ACT.Gelu, bias=pack_sb[:, C_B1:C_B1 + 1]).then_inc(m2_done, 1)
            act.wait_ge(eps_done, 1)
            nc.scalar.activation(vcol[:], vcol2[:], ACT.Ln).then_inc(vlog_done, 1)
            act.wait_ge(am_max_done, 1)
            nc.scalar.activation(am_exp[:], am[:], ACT.Exp, bias=am_max[:], accum_out=am_sum[:]).then_inc(am_exp_done, 1)
            act.wait_ge(ld_w0, 16)
            nc.scalar.copy(w0_hi[:, :, Z0N:Z0N + D], w0_sb[:]).then_inc(w0_hi_done, 1)
            act.wait_ge(a0_mm, 1)
            nc.scalar.copy(w0_hi[:, :, 0:Z0N], p_h1[:, 0:HC * Z0N].rearrange("p (c n) -> p c n", c=HC)).then_inc(a0_hi_done, 1)
            act.wait_ge(mix_mm, 1)
            act.wait_ge(mix_zeroed, 1)
            for b in range(BT):
                rows = slice(b * CH, (b + 1) * CH)
                nc.scalar.copy(mix[rows, :, b * CH:b * CH + CH // 2],
                               p_cv[rows, :].rearrange("p (o t) -> p t o", t=NT)).then_inc(mix_a_done, 1)
            act.wait_ge(b0_mm, 1)
            nc.scalar.copy(b0_round[:], p_y1[0:K0, :]).then_inc(b0_round_done, 1)

            def step(s):
                if s.live():
                    after(act, z0_nmax_done, s)
                    nc.scalar.activation(z0_exp[:], z0[:, L0N:Z0N], ACT.Exp, bias=z0_nmax[:],
                                         accum_out=z0_sum[:]).then_inc(z0_exp_done, 1)
                if (s + -LAG).live():
                    after(act, cv_mm, s, -LAG)
                    nc.scalar.copy(cv[:], p_cv[:]).then_inc(cv_done, 1)
                if (s + 1).live():
                    t = s + 1
                    after(act, c0_mm, t)
                    nc.scalar.copy(c0_hi[:, t.mod(2), :], p_c0[:]).then_inc(c0_hi_done, 1)
                if s.live():
                    after(act, g0_tr, s)
                    nc.scalar.copy(g0t[:], p_g0t).then_inc(g0t_done, 1)
                if (s + -3).live():
                    after(act, g1_tr, s, -3)
                    nc.scalar.copy(g1t_hi[:], p_g1t).then_inc(g1t_hi_done, 1)
                if (s + -LAG).live():
                    after(act, c1_tr, s, -LAG)
                    nc.scalar.copy(c1_hi[:].rearrange("p r (a o) -> p a r o", o=GC),
                                   p_c1[:].rearrange("p (a r o) -> p a r o", r=NPH, o=GC)).then_inc(c1_hi_done, 1)
                if s.i is None and s.c == 0:
                    act.wait_ge(ld_a1, 16)
                    nc.scalar.copy(a1_hi[:], a1_sb[:]).then_inc(a1_hi_done, 1)
                    act.wait_ge(ld_w1, 16)
                    nc.scalar.copy(w1_hi[:], w1_sb[:]).then_inc(w1_hi_done, 1)
                if s.i is None and s.c == 1:
                    for a in range(2):
                        act.wait_ge(b1_mm, a + 1)
                        nc.scalar.copy(b1_hi[:, a, :], (p_cv, p_h1)[a][0:K1, :]).then_inc(b1_hi_done, 1)
                if (s + -LAG).live():
                    after(act, ntop_done, s, -LAG)
                    nc.scalar.activation(t_exp[:], top[:, 0:2], ACT.Exp, bias=ntop[:],
                                         accum_out=t_sum[:]).then_inc(t_exp_done, 1)

            steps(act, step, -1, NT + 2, 3, 7)

        @block.vector
        def _(dve):
            V = nc.vector
            dve.wait_ge(ld_pack, 16)
            dve.wait_ge(ident_done, 1)
            V.tensor_reduce(mask_c[:], ident[:].rearrange("p (t c) -> p c t", c=BT), X, ALU.add).then_inc(masks_done, 1)
            V.tensor_reduce(mask_t[:], ident[:].rearrange("p (t c) -> p t c", c=BT), X, ALU.add).then_inc(masks_done, 1)
            V.memset(ones_r[:].bitcast(f32), 1.0).then_inc(ones_done, 1)
            V.memset(pick_rs0[:].bitcast(f32), 0.0).then_inc(picks_zeroed, 1)
            V.memset(pick_bias[:], 0.0).then_inc(picks_zeroed, 1)
            V.memset(pick_rs1[:].bitcast(f32), 0.0).then_inc(picks_zeroed, 1)
            V.memset(sel[:], 0.0).then_inc(sel_zeroed, 1)
            dve.wait_ge(picks_zeroed, 3)
            V.memset(pick_rs0[:, 3 * L0N:3 * L0N + 3].bitcast(f32), 1.0).then_inc(picks_done, 1)
            V.memset(pick_bias[:, 3 * L0N + 3:K0], 1.0).then_inc(picks_done, 1)
            V.memset(pick_rs1[:, HB:K1].bitcast(f32), 1.0).then_inc(picks_done, 1)
            dve.wait_ge(ld_act, 16)
            dve.wait_ge(iotas_done, 3)
            V.tensor_scalar(act8[:], act_sb[:], float(R), None, ALU.mult).then_inc(act8_done, 1)
            V.tensor_copy(iota_e[:], iota_e_i[:]).then_inc(iota_e_done, 1)
            V.tensor_tensor(sel_r[:], iota_row[:], act_sb[0:E0, :], ALU.is_equal).then_inc(sel_r_done, 1)
            dve.wait_ge(act8_done, 1)
            dve.wait_ge(sel_zeroed, 1)
            for n in range(3):
                V.tensor_tensor(sel[:, n * L0N:(n + 1) * L0N].rearrange("p (s r) -> p s r", r=R), iota_slot[:],
                                act8[:].unsqueeze(2).to_broadcast([P, ACT0, R]), ALU.is_equal).then_inc(sel_done, 1)
            dve.wait_ge(ld_rt, 16)
            V.tensor_scalar(vcol2[:], rt_sb[:, D + 1:D + 2], EPS, None, ALU.add).then_inc(eps_done, 1)
            dve.wait_ge(am_mm, 1)
            V.tensor_tensor(am[:], p_g[:, 0:MK], pack_sb[:, C_B2:C_B2 + MK], ALU.add).then_inc(am_done, 1)
            dve.wait_ge(am_done, 1)
            V.tensor_reduce(am_max[:], am[:], X, ALU.max, negate=True).then_inc(am_max_done, 1)
            dve.wait_ge(beta1_mm, 1)
            V.tensor_scalar(beta1[:], p_c1[:, 0:NT], pack_sb[:, C_FS:C_FS + 1], None, ALU.add).then_inc(beta1_done, BT)
            dve.wait_ge(am_exp_done, 1)
            V.reciprocal(am_rec[:], am_sum[:]).then_inc(am_rec_done, 1)
            dve.wait_ge(am_rec_done, 1)
            V.tensor_scalar(att[:], am_exp[:], am_rec[:], None, ALU.mult).then_inc(att_done, 1)
            dve.wait_ge(att_done, 1)
            dve.wait_ge(masks_done, 2)
            V.tensor_tensor(att_m[:], att[:].unsqueeze(1).to_broadcast([P, BT, MK]),
                            mask_c[:].unsqueeze(2).to_broadcast([P, BT, MK]), ALU.mult).then_inc(att_m_done, 1)
            dve.wait_ge(att_t_mm, 1)
            V.tensor_copy(att_t[:], p_g[0:BT * MK, 0:NT]).then_inc(att_t_done, 1)
            dve.wait_ge(a0_hi_done, 1)
            V.tensor_tensor(w0_lo[:, :, 0:Z0N], p_h1[:, 0:HC * Z0N].rearrange("p (c n) -> p c n", c=HC),
                            w0_hi[:, :, 0:Z0N].bitcast(f32), ALU.subtract).then_inc(a0_lo_done, 1)
            dve.wait_ge(w0_hi_done, 1)
            V.tensor_tensor(w0_lo[:, :, Z0N:Z0N + D], w0_sb[:], w0_hi[:, :, Z0N:Z0N + D].bitcast(f32),
                            ALU.subtract).then_inc(w0_lo_done, 1)
            dve.wait_ge(mix_mm, 1)
            dve.wait_ge(mix_zeroed, 1)
            for b in range(BT):
                rows = slice(b * CH, (b + 1) * CH)
                V.tensor_copy(mix[rows, :, b * CH + CH // 2:(b + 1) * CH],
                              p_y0b[rows, :].rearrange("p (o t) -> p t o", t=NT)).then_inc(mix_b_done, 1)
            dve.wait_ge(beta0_mm, 1)
            V.tensor_copy(beta0[:], p_c1[:, 0:NT]).then_inc(beta0_done, 1)
            V.memset(beta5[:, :, 3:5], 1.0).then_inc(beta5_ones, 1)
            dve.wait_ge(beta0_done, 1)
            V.tensor_copy(beta5[:, :, 0].bitcast(f32r), beta0[:]).then_inc(beta5_hi, 1)
            dve.wait_ge(beta5_hi, 1)
            V.tensor_tensor(beta5[:, :, 1], beta0[:], beta5[:, :, 0], ALU.subtract).then_inc(beta5_lo, 1)
            dve.wait_ge(beta5_lo, 1)
            dve.wait_ge(beta5_ones, 1)
            V.tensor_copy(beta5[:, :, 2], beta5[:, :, 0]).then_inc(beta5_done, 1)
            dve.wait_ge(vlog_done, 1)
            V.tensor_tensor(vmat[:, 0:1], vcol[:], rt_sb[:, D:D + 1], ALU.add).then_inc(vcol2_done, 1)
            dve.wait_ge(vcol2_done, 1)
            V.tensor_copy(vmat[:, 1:P], vmat[:, 0:1].to_broadcast([E0, P - 1])).then_inc(vmat_done, 1)
            dve.wait_ge(rs0_mm, 1)
            V.tensor_copy(rs0[:], p_h1[:, 0:Z0N]).then_inc(rs0_done, 1)
            dve.wait_ge(vrow_mm, 1)
            V.tensor_copy(vrow[:], p_h1[:, 0:ACT0]).then_inc(vrow_done, 1)
            dve.wait_ge(rs0_done, 1)
            V.tensor_tensor(z_add[:], rs0[:].unsqueeze(1).to_broadcast([P, NT, Z0N]),
                            beta0[:].unsqueeze(2).to_broadcast([P, NT, Z0N]), ALU.mult).then_inc(z_mul_done, 1)
            dve.wait_ge(z_mul_done, 1)
            dve.wait_ge(vrow_done, 1)
            V.tensor_tensor(z_add[:, :, L0N:Z0N], z_add[:, :, L0N:Z0N],
                            vrow[:].unsqueeze(1).to_broadcast([P, NT, ACT0]), ALU.add).then_inc(z_add_done, 1)
            dve.wait_ge(b0_round_done, 1)
            dve.wait_ge(lomask_done, 1)
            V.scalar_tensor_tensor(b0_stack[:], b0_round[:].bitcast(f32), minus_lo_row[0:K0], p_y1[0:K0, :],
                                   ALU.mult, ALU.add).then_inc(b0_done, 1)

            def step(s):
                if s.live():
                    after(dve, z0_mm, s)
                    if s.i is None and s.c == 0:
                        dve.wait_ge(z_add_done, 1)
                    V.tensor_tensor(z0[:], p_y0a[:, 0:Z0N], z_add[:, s.n(), :], ALU.add).then_inc(z0_done, 1)
                    after(dve, z0_done, s)
                    V.tensor_reduce(z0_nmax[:], z0[:, L0N:Z0N], X, ALU.max, negate=True).then_inc(z0_nmax_done, 1)
                    after(dve, z0_exp_done, s)
                    V.reciprocal(z0_rec[:], z0_sum[:]).then_inc(z0_rec_done, 1)
                    after(dve, z0_rec_done, s)
                    V.tensor_scalar(alpha[:], z0_exp[:], z0_rec[:], SCALING, ALU.mult, ALU.mult).then_inc(alpha_done, 1)
                    after(dve, alpha_done, s)
                    V.tensor_tensor(g0[:].rearrange("p (s r) -> p s r", r=R), z0[:, 0:L0N].rearrange("p (s r) -> p s r", r=R),
                                    alpha[:].unsqueeze(2).to_broadcast([P, ACT0, R]), ALU.mult).then_inc(g0_done, 1)
                    after(dve, g0_done, s)
                    after(dve, g0_tr, s, -1)
                    V.tensor_copy(g0s[:, 0:3 * L0N].rearrange("p (a n) -> p a n", n=L0N)[:, 0:3:2, :].bitcast(f32r),
                                  g0[:].unsqueeze(1).to_broadcast([P, 2, L0N])).then_inc(g0_hi_done, 1)
                    after(dve, g0_hi_done, s)
                    V.tensor_tensor(g0s[:, L0N:2 * L0N], g0[:], g0s[:, 0:L0N], ALU.subtract).then_inc(g0_lo_done, 1)
                if (s + 1).live():
                    t = s + 1
                    after(dve, c0_hi_done, t)
                    V.tensor_tensor(c0_lo[:, t.mod(2), :], p_c0[:], c0_hi[:, t.mod(2), :].bitcast(f32),
                                    ALU.subtract).then_inc(c0_lo_done, 1)
                if (s + -3).live():
                    after(dve, g1t_hi_done, s, -3)
                    V.tensor_tensor(g1t_lo[:], p_g1t, g1t_hi[:].bitcast(f32), ALU.subtract).then_inc(g1t_lo_done, 1)
                if (s + -LAG).live():
                    after(dve, c1_hi_done, s, -LAG)
                    V.tensor_tensor(c1_lo[:].rearrange("p r (a o) -> p a r o", o=GC),
                                    p_c1[:].rearrange("p (a r o) -> p a r o", r=NPH, o=GC),
                                    c1_hi[:].bitcast(f32).rearrange("p r (a o) -> p a r o", o=GC),
                                    ALU.subtract).then_inc(c1_lo_done, 1)
                if (s + -3).live():
                    v = s + -3
                    after(dve, y1_mm, v)
                    after_dma(dve, y_stored, v, -2)
                    V.tensor_tensor(y_sb[:, v.mod(2), :].rearrange("p (q f) -> p f q", f=NPH),
                                    p_y1[:].rearrange("p (f q) -> p f q", f=NPH), x1[:, v.mod(4), :, 1:1 + NQ],
                                    ALU.add).then_inc(y_done, 1)
                if s.live():
                    after(dve, y0_mm, s)
                    after_dma(dve, x1_stored, s, -4)
                    for n in range(2):
                        phases = slice(n * NPH // 2, (n + 1) * NPH // 2)
                        last = V.tensor_tensor(x1[:, s.mod(4), phases, 1:1 + NQ], p_y0[n].rearrange("p (f q) -> p f q", q=NQ),
                                               x_sb[:, s.mod(4), :].rearrange("p (q f) -> p f q", f=NPH)[:, phases, :], ALU.add)
                    last.then_inc(x1_done, 1)
                if s.i is None and s.c == 0:
                    dve.wait_ge(a1_hi_done, 1)
                    V.tensor_tensor(a1_lo[:], a1_sb[:], a1_hi[:].bitcast(f32), ALU.subtract).then_inc(a1_lo_done, 1)
                    dve.wait_ge(w1_hi_done, 1)
                    V.tensor_tensor(w1_lo[:], w1_sb[:], w1_hi[:].bitcast(f32), ALU.subtract).then_inc(w1_lo_done, 1)
                if s.i is None and s.c == 1:
                    for a in range(2):
                        dve.wait_ge(b1_hi_done, a + 1)
                        V.tensor_tensor(b1_lo[:, a, :], (p_cv, p_h1)[a][0:K1, :], b1_hi[:, a, :].bitcast(f32),
                                        ALU.subtract).then_inc(b1_lo_done, 1)
                    dve.wait_ge(rs1_mm, 1)
                    V.tensor_copy(rs1[:], p_c1[:, 0:H1N]).then_inc(rs1_done, 1)
                if (s + -LAG).live():
                    v = s + -LAG
                    after(dve, h1_mm, v)
                    if v.i is None and v.c == 0:
                        dve.wait_ge(rs1_done, 1)
                        dve.wait_ge(beta1_done, BT)
                        dve.wait_ge(iota_e_done, 1)
                    beta = beta1[:, bass.ds(v.n(), 1)]
                    V.scalar_tensor_tensor(h1[:, L1N:H1N], rs1[:, L1N:H1N], beta, p_h1[:, L1N:H1N],
                                           ALU.mult, ALU.add).then_inc(logits_done, 1)
                    after(dve, logits_done, v)
                    V.scalar_tensor_tensor(h1[:, 0:L1N], rs1[:, 0:L1N], beta, p_h1[:, 0:L1N],
                                           ALU.mult, ALU.add).then_inc(h1_done, 1)
                    V.max(top[:], h1[:, L1N:H1N]).then_inc(top_done, 1)
                    after(dve, top_done, v)
                    V.tensor_scalar(ntop[:], top[:, 0:1], -1.0, None, ALU.mult).then_inc(ntop_done, 1)
                    V.max_index(top_i[:], top[:], h1[:, L1N:H1N]).then_inc(top_i_done, 1)
                    after(dve, top_i_done, v)
                    V.tensor_copy(top_f[:], top_i[:, 0:2]).then_inc(top_f_done, 1)
                    after(dve, t_exp_done, v)
                    V.reciprocal(t_rec[:], t_sum[:]).then_inc(t_rec_done, 1)
                    after(dve, t_rec_done, v)
                    V.tensor_scalar(prob[:], t_exp[:], t_rec[:], SCALING, ALU.mult, ALU.mult).then_inc(prob_done, 1)
                    after(dve, prob_done, v)
                    after(dve, top_f_done, v)
                    V.tensor_scalar(gate_a[:], iota_e[:], top_f[:, 0:1], prob[:, 0:1], ALU.is_equal, ALU.mult).then_inc(gate_a_done, 1)
                    V.tensor_scalar(gate_b[:], iota_e[:], top_f[:, 1:2], prob[:, 1:2], ALU.is_equal, ALU.mult).then_inc(gate_b_done, 1)
                    after(dve, gate_a_done, v)
                    after(dve, gate_b_done, v)
                    V.tensor_tensor(gate[:], gate_a[:], gate_b[:], ALU.add).then_inc(gate_done, 1)
                    after(dve, gate_done, v)
                    after(dve, h1_done, v)
                    after(dve, g1_tr, v, -1)
                    V.tensor_tensor(g1[:, :, 0:HB].rearrange("p a (e r) -> p a e r", r=R),
                                    h1[:, 0:L1N].rearrange("p (a e r) -> p a e r", a=2, r=R),
                                    gate[:].rearrange("p (a e) -> p a e", a=2).unsqueeze(3).to_broadcast([P, 2, E1 // 2, R]),
                                    ALU.mult).then_inc(g1_done, 1)

            dve.wait_ge(x1_padded, 2)
            steps(dve, step, -1, NT + 2, 3, 7)

        @block.tensor
        def _(pe):
            mm = nc.tensor.matmul

            def hi_passes(psum, operands, start):
                for n, (lhs_hi, _, rhs_hi, rhs_lo) in enumerate(operands):
                    mm(psum, lhs_hi, rhs_hi, start=start and n == 0, stop=False)
                    mm(psum, lhs_hi, rhs_lo, start=False, stop=False)

            def lo_passes(psum, operands, stop):
                for n, (_, lhs_lo, rhs_hi, _) in enumerate(operands):
                    last = mm(psum, lhs_lo, rhs_hi, start=False, stop=stop and n == len(operands) - 1)
                return last

            pe.wait_ge(ld_pack, 16)
            cond = pack_sb[:, C_COND:C_COND + BATCH]
            mm(p_c0[:, 0:P], pack_sb[:, C_W0:C_W0 + P], cond, start=True, stop=True).then_inc(u1_mm, 1)
            for b in range(BT):
                last = mm(p_c1[b * CH:(b + 1) * CH, 0:NT], pack_sb[:, C_CW:C_CW + CH],
                          cond.rearrange("p (t b) -> p b t", b=BT)[:, b, :], start=True, stop=True)
            last.then_inc(beta1_mm, 1)
            pe.wait_ge(m1_done, 1)
            mm(p_c0[:, 0:P], pack_sb[:, C_W1:C_W1 + P], m1[:], start=True, stop=True).then_inc(u2_mm, 1)
            pe.wait_ge(m2_done, 1)
            mm(p_g[:, 0:MK], m2[:], pack_sb[:, C_W2:C_W2 + MK], start=True, stop=True).then_inc(am_mm, 1)
            pe.wait_ge(sel_done, 3)
            pe.wait_ge(sel_r_done, 1)
            pe.wait_ge(ld_exp, 16)
            pe.wait_ge(ld_rt, 16)
            for c in range(HC):
                mm(p_h1[:, c * Z0N:c * Z0N + L0N], exp_sb[:, 0, c * P:(c + 1) * P], sel[:, 0:L0N], start=True, stop=True)
                last = mm(p_h1[:, c * Z0N + L0N:(c + 1) * Z0N], rt_sb[:, c * P:(c + 1) * P], sel_r[:], start=True, stop=True)
            last.then_inc(a0_mm, 1)
            pe.wait_ge(att_m_done, 1)
            mm(p_g[0:BT * MK, 0:NT], att_m[:].rearrange("p b k -> p (b k)"), mask_t[:], start=True, stop=True).then_inc(att_t_mm, 1)
            pe.wait_ge(att_t_done, 1)
            pe.wait_ge(ld_kw, 16)
            for o in range(CH):
                bank = (p_cv, p_y0b)[o // 16]
                last = mm(bank[:, (o % 16) * NT:(o % 16 + 1) * NT], kw_sb[:, o, :], att_t[:], start=True, stop=True)
            last.then_inc(mix_mm, 1)
            pe.wait_ge(beta1_done, BT)
            mm(p_c1[:, 0:NT], kw_sb[:, CH, :], att_t[:], start=True, stop=True).then_inc(beta0_mm, 1)
            pe.wait_ge(a0_lo_done, 1)
            pe.wait_ge(ones_done, 1)
            for c in range(HC):
                for h, half in enumerate((w0_hi, w0_lo)):
                    last = mm(p_h1[:, 0:Z0N], ones_r[:], half[:, c, 0:Z0N], start=(c + h == 0), stop=(c == HC - 1 and h == 1))
            last.then_inc(rs0_mm, 1)
            pe.wait_ge(rs0_done, 1)
            pe.wait_ge(vmat_done, 1)
            mm(p_h1[:, 0:ACT0], vmat[:], sel_r[:], start=True, stop=True).then_inc(vrow_mm, 1)
            pe.wait_ge(w0_lo_done, 1)
            pe.wait_ge(picks_done, 3)
            pe.wait_ge(ld_bb, 16)
            mm(p_y1[0:K0, :], sel[:], exp_sb[:, 1, :], start=True, stop=False)
            for c in range(HC):
                mm(p_y1[0:K0, :], pick_rs0[:], w0_hi[:, c, Z0N:Z0N + D], start=False, stop=False)
                mm(p_y1[0:K0, :], pick_rs0[:], w0_lo[:, c, Z0N:Z0N + D], start=False, stop=False)
            mm(p_y1[0:K0, :], pick_bias[:], bb_sb[:], start=False, stop=True).then_inc(b0_mm, 1)
            pe.wait_ge(mix_a_done, BT)
            pe.wait_ge(mix_b_done, BT)

            def step(s):
                c0_pairs = [(c0_hi[:, s.mod(2), c * P:(c + 1) * P], c0_lo[:, s.mod(2), c * P:(c + 1) * P]) for c in range(HC)]
                if s.live():
                    after(pe, c0_lo_done, s)
                    after(pe, x1_done, s, -1)
                    first = [(*c0_pairs[c], w0_hi[:, c, 0:Z0N + NY], w0_lo[:, c, 0:Z0N + NY]) for c in range(HC)]
                    hi_passes(p_y0a[:, 0:Z0N + NY], first, True)
                    lo_passes(p_y0a[:, 0:Z0N + NY], first, True).then_inc(z0_mm, 1)
                if (s + -LAG).live():
                    v = s + -LAG
                    after_dma(pe, win_loaded, v, 0, 16 * (WIN // NPH))
                    after(pe, cv_done, v, -1)
                    if v.i is None and v.c == 0:
                        pe.wait_ge(ld_wc, 16)
                        pe.wait_ge(b1_hi_done, 2)
                        pe.wait_ge(b1_lo_done, 2)
                    for g in range(GROUPS):
                        last = mm(p_cv[g * CH:(g + 1) * CH, :], wc_sb[:, g, :],
                                  win[:, v.mod(2)].rearrange("p (b g) q -> p g b q", g=GROUPS)[:, g], start=True, stop=True)
                    last.then_inc(cv_mm, 1)
                if (s + 1).live():
                    t = s + 1
                    after_dma(pe, x_loaded, t)
                    after(pe, c0_lo_done, s)
                    for c in range(HC):
                        cols = slice(c * P, (c + 1) * P)
                        last = mm(p_c0[:, cols], x_sb[:, t.mod(4), cols], mix[:, t.n(), :], start=True, stop=True)
                    last.then_inc(c0_mm, 1)
                if (s + -LAG).live():
                    v = s + -LAG
                    after(pe, cv_done, v)
                    after(pe, c1_lo_done, v, -1)
                    if v.i is None and v.c == 0:
                        pe.wait_ge(rs1_done, 1)
                    for b in range(BT):
                        cols = slice(b * P, (b + 1) * P)
                        last = nc.tensor.transpose(p_c1[:, cols], cv[:, cols], ident[:])
                    last.then_inc(c1_tr, 1)
                if (s + -3).live():
                    v = s + -3
                    after(pe, g1_done, v)
                    after(pe, g1_beta_done, v)
                    after(pe, g1t_lo_done, v, -1)
                    after(pe, g0t_done, s, -1)
                    if v.i is None and v.c == 0:
                        pe.wait_ge(g1_padded, 1)
                    for a in range(2):
                        last = nc.tensor.transpose(p_g1t[:, a, :], g1[:, a, :], ident[:])
                    last.then_inc(g1_tr, 1)
                if s.live():
                    after(pe, g0_lo_done, s)
                    after(pe, g0_beta_done, s)
                    after(pe, g0t_done, s, -1)
                    nc.tensor.transpose(p_g0t, g0s[:], ident[:]).then_inc(g0_tr, 1)
                    other = [(*c0_pairs[c], w0_hi[:, c, Z0N + NY:Z0N + D], w0_lo[:, c, Z0N + NY:Z0N + D]) for c in range(HC)]
                    hi_passes(p_y0[1], other, True)
                    lo_passes(p_y0[1], other, False)
                if (s + -3).live():
                    ranks = [(g1t_hi[:, a, :], g1t_lo[:, a, :], b1_hi[:, a, :], b1_lo[:, a, :]) for a in range(2)]
                    after(pe, g1t_hi_done, s, -3)
                    hi_passes(p_y1[:], ranks, False)
                    after(pe, g1t_lo_done, s, -3)
                    lo_passes(p_y1[:], ranks, True).then_inc(y1_mm, 1)
                if s.live():
                    after(pe, g0t_done, s)
                    mm(p_y0[0], g0t[:], b0_stack[:, 0:NY], start=False, stop=True, skip_group_check=True)
                    last = mm(p_y0[1], g0t[:], b0_stack[:, NY:D], start=False, stop=True)
                    last.then_inc(y0_mm, 1)
                if s.i is None and s.c == 0:
                    pe.wait_ge(ld_b1, 16)
                    mm(p_cv[0:K1, :], ident[0:HB, 0:K1], b1_sb[:, 0, :], start=True, stop=True).then_inc(b1_mm, 1)
                    mm(p_h1[0:K1, :], ident[0:HB, 0:K1], b1_sb[:, 1, :], start=True, stop=False)
                    pe.wait_ge(w1_lo_done, 1)
                    for c in range(HC):
                        mm(p_h1[0:K1, :], pick_rs1[:], w1_hi[:, c, :], start=False, stop=False)
                        last = mm(p_h1[0:K1, :], pick_rs1[:], w1_lo[:, c, :], start=False, stop=(c == HC - 1))
                    last.then_inc(b1_mm, 1)
                    for c in range(HC):
                        mm(p_c1[:, 0:H1N], ones_r[:], a1_hi[:, c, :], start=(c == 0), stop=False)
                        last = mm(p_c1[:, 0:H1N], ones_r[:], a1_lo[:, c, :], start=False, stop=(c == HC - 1))
                    last.then_inc(rs1_mm, 1)
                if (s + -LAG).live():
                    v = s + -LAG
                    lows = [(c1_hi[:, c, :], c1_lo[:, c, :], a1_hi[:, c, :], a1_lo[:, c, :]) for c in range(HC)]
                    full = [(c1_hi[:, c, :], c1_lo[:, c, :], w1_hi[:, c, :], w1_lo[:, c, :]) for c in range(HC)]
                    after(pe, c1_hi_done, v)
                    after(pe, h1_done, v, -1)
                    hi_passes(p_h1[:, 0:H1N], lows, True)
                    after(pe, c1_lo_done, v)
                    lo_passes(p_h1[:, 0:H1N], lows, True).then_inc(h1_mm, 1)
                    after(pe, y_done, v, -1)
                    hi_passes(p_y1[:], full, True)
                    lo_passes(p_y1[:], full, False)

            steps(pe, step, -1, NT + 2, 3, 7)


def by_phase(a):
    return np.ascontiguousarray(a.reshape(*a.shape[:-1], NQ, NPH).swapaxes(-1, -2)).reshape(a.shape)


def lay_out(i):
    f = np.float32
    pack = np.zeros((P, C_END), f)
    pack[:, C_COND:C_COND + BATCH] = i["cond_128"].T
    pack[:, C_W0:C_W0 + P] = i["L0_cond_W0"]
    pack[:, C_W1:C_W1 + P] = i["L0_cond_W1"]
    pack[:, C_W2:C_W2 + MK] = i["L0_cond_W2"]
    pack[:, C_B2:C_B2 + MK] = i["L0_cond_b2"][None, :]
    pack[:, C_B0] = i["L0_cond_b0"]
    pack[:, C_B1] = i["L0_cond_b1"]
    pack[:, C_FS] = np.tile(i["fside_S_0"], BT)
    pack[:, C_CW:C_CW + CH] = i["L1_cond_c_weight"].T
    kw = np.zeros((BT, MK, CH + 1, BT, CH), f)
    for b in range(BT):
        kw[b, :, :CH, b, :] = i["L0_cond_weight"][..., 0]
        kw[b, :, CH, b, :] = i["L0_cond_bias_k"]
    experts = np.stack([i["L0_ffn_lora_A"].reshape(P, D),
                        by_phase(i["L0_ffn_lora_B"].transpose(0, 2, 1).reshape(P, D))], 1)
    router = np.concatenate([i["L0_ffn_router_W"], i["L0_ffn_router_b"][:, None], i["L0_ffn_domain_prior"][:, None]], 1)
    w0 = by_phase(i["L0_ffn_W_base"].T).reshape(HC, P, D).transpose(1, 0, 2)
    w1 = by_phase(i["L1_ffn_base_W"].T).reshape(NQ, NPH * D)
    a1 = np.concatenate([i["L1_ffn_lora_A"].reshape(L1N, D), i["L1_ffn_gate_W"]], 0).T.reshape(NQ, NPH * H1N)
    b1 = by_phase(i["L1_ffn_lora_B"].transpose(0, 2, 1).reshape(L1N, D)).reshape(2, HB, D).transpose(1, 0, 2)
    wc = np.zeros((WIN // NPH, GC, NPH, GROUPS, NPH, GC), f)
    w = i["L1_cond_weight"].reshape(GROUPS, GC, GC, TAPS)
    for s in range(WIN):
        for r in range(NPH):
            if 0 <= s - r < TAPS:
                wc[s // NPH, :, s % NPH, :, r, :] = w[:, :, :, s - r].transpose(2, 0, 1)
    c = np.ascontiguousarray
    return {
        "x": c(i["x"]), "pack": pack, "kw": c(kw.reshape(BT * MK, -1)), "experts": c(experts.reshape(P, -1)),
        "router": c(router), "active": c(np.broadcast_to(i["L0_ffn_active"], (P, ACT0))),
        "b_base": c(by_phase(i["L0_ffn_b_base"])[None, :]), "w0": c(w0.reshape(P, -1)), "w1": c(w1), "a1": c(a1),
        "b1": c(b1.reshape(HB, -1)), "wc": c(wc.reshape(KIM, -1)),
    }


def kernel(**inputs):
    import concourse.bacc as bacc
    from concourse.bass_utils import run_bass_kernel_spmd

    arrays = lay_out({k: np.asarray(v) for k, v in inputs.items()})
    nc = bacc.Bacc("TRN2", target_bir_lowering=False, num_devices=1)
    args = {n: nc.dram_tensor(f"in_{n}", a.shape, mybir.dt.from_np(a.dtype), kind="ExternalInput").ap()
            for n, a in arrays.items()}
    out = nc.dram_tensor("out", (BATCH, CH, D), mybir.dt.float32, kind="ExternalOutput").ap()
    build(nc, out=out, **args)
    r = run_bass_kernel_spmd(nc, [{f"in_{n}": a for n, a in arrays.items()}], core_ids=[0])
    return r.results[0]["out"]
```

```python
import numpy as np

import concourse.bass as bass
from concourse import mybir
from contextlib import ExitStack

P = 128
BATCH, CH, D = 128, 32, 512
BT = P // CH
NT = BATCH // BT
HC = D // P
NPH, NQ = 4, D // 4
GROUPS, GC, TAPS = 4, 8, 9
CG = BT * GROUPS
WIN = 12
KIM = WIN * GC
NQP = NQ + 2
E0, ACT0, R = 16, 4, 8
L0N = ACT0 * R
Z0N = L0N + ACT0
E1 = 28
L1N = E1 * R
H1N = L1N + E1
HB = L1N // 2
K1 = HB + 1
K0 = 3 * L0N + 5
MK = 8
KM = 3 * MK
SCALING = 2.0
EPS = 1e-12
UNROLL, LAG = 4, 2

C_COND, C_W0, C_W1, C_W2, C_B2, C_B0, C_B1, C_FS, C_CW = 0, 128, 256, 384, 392, 400, 401, 402, 403
C_END = C_CW + CH


class Tile:

    def __init__(self, i, c):
        self.i, self.c = i, c

    def __add__(self, n):
        return Tile(self.i, self.c + n)

    def n(self):
        return self.c if self.i is None else self.i * UNROLL + self.c

    def mod(self, m):
        return self.c % m

    def over(self, m):
        return self.c // m if self.i is None else self.i * (UNROLL // m) + self.c // m

    def live(self):
        return self.i is not None or 0 <= self.c < NT


def steps(engine, step, first, last, loop_from, loops):
    for c in range(first, loop_from):
        step(Tile(None, c))
    with engine.Fori(0, loops) as i:
        for u in range(UNROLL):
            step(Tile(i, loop_from + u))
    for c in range(loop_from + loops * UNROLL, last + 1):
        step(Tile(None, c))


def build(nc, x, pack, kw, experts, router, active, b_base, w0, w1, a1, b1, wc, out):
    f32, f32r, i32, u32 = mybir.dt.float32, mybir.dt.float32r, mybir.dt.int32, mybir.dt.uint32
    ALU = mybir.AluOpType
    ACT = mybir.ActivationFunctionType
    X = mybir.AxisListType.X

    ctx = ExitStack()
    with ctx:
        def sb(name, shape, dt=f32):
            return ctx.enter_context(nc.sbuf_tensor(name, shape, dt))

        def pb(name):
            return ctx.enter_context(nc.psum_tensor(name, [P, 512], f32))

        def sem(name):
            return ctx.enter_context(nc.semaphore(name))

        scratch = nc.dram_tensor("x1_scratch", (NT, P, NPH, NQP), f32, kind="Internal").ap()

        pack_sb = sb("pack_sb", [P, C_END])
        kw_sb = sb("kw_sb", [KM, CH * CH + CH])
        kw_round = sb("kw_round", [KM, CH * CH + CH], f32r)
        kw_stack = sb("kw_stack", [KM, CH * CH + CH], f32r)
        exp_sb = sb("exp_sb", [P, 2, D])
        rt_sb = sb("rt_sb", [E0, D + 2])
        act_sb = sb("act_sb", [P, ACT0], i32)
        bb_sb = sb("bb_sb", [1, D])
        w0_sb = sb("w0_sb", [P, HC, D])
        w1_sb = sb("w1_sb", [P, HC, D])
        a1_sb = sb("a1_sb", [P, HC, H1N])
        b1_sb = sb("b1_sb", [HB, 2, D])
        wc_sb = sb("wc_sb", [KIM, GROUPS, NPH * GC])
        w0_hi = sb("w0_hi", [P, HC, Z0N + D], f32r)
        w0_lo = sb("w0_lo", [P, HC, Z0N + D], f32r)
        w1_hi = sb("w1_hi", [P, HC, D], f32r)
        w1_lo = sb("w1_lo", [P, HC, D], f32r)
        a1_hi = sb("a1_hi", [P, HC, H1N], f32r)
        a1_lo = sb("a1_lo", [P, HC, H1N], f32r)
        b0_round = sb("b0_round", [K0, D], f32r)
        b0_stack = sb("b0_stack", [K0, D], f32r)
        b1_hi = sb("b1_hi", [K1, 2, D], f32r)
        b1_lo = sb("b1_lo", [K1, 2, D], f32r)
        mix = sb("mix", [P, NT, P])

        ident = sb("ident", [P, P])
        ones = sb("ones", [P, P])
        pick_rs0 = sb("pick_rs0", [P, K0])
        pick_bias = sb("pick_bias", [1, K0])
        pick_rs1 = sb("pick_rs1", [P, K1])
        minus_lo_row = sb("minus_lo_row", [P, 1])
        minus_lo_kw = sb("minus_lo_kw", [P, 1])
        iota_slot = sb("iota_slot", [P, ACT0, R], i32)
        iota_row = sb("iota_row", [E0, ACT0], i32)
        iota_e_i = sb("iota_e_i", [P, E1], i32)
        iota_e = sb("iota_e", [P, E1])
        act8 = sb("act8", [P, ACT0])
        w_pair = sb("w_pair", [P, 2, D])
        w0_sum = sb("w0_sum", [P, D])
        w1_sum = sb("w1_sum", [P, D])
        a1_pair = sb("a1_pair", [P, 2, H1N])
        a1_sum = sb("a1_sum", [P, H1N])
        a0_sum = sb("a0_sum", [P, Z0N])
        sel = sb("sel", [P, K0])
        sel_r = sb("sel_r", [E0, ACT0])

        m1 = sb("m1", [P, BATCH])
        m2 = sb("m2", [P, BATCH])
        am = sb("am", [P, MK])
        am_max = sb("am_max", [P, 1])
        am_exp = sb("am_exp", [P, MK])
        am_sum = sb("am_sum", [P, 1])
        am_rec = sb("am_rec", [P, 1])
        att = sb("att", [P, MK])
        att3 = sb("att3", [P, 3, MK])
        att_t = sb("att_t", [KM, BATCH], f32r)
        beta0 = sb("beta0", [P, NT])
        beta1 = sb("beta1", [P, NT])
        beta5 = sb("beta5", [P, NT, 5])
        rs0 = sb("rs0", [P, Z0N])
        vcol = sb("vcol", [E0, 1])
        vcol2 = sb("vcol2", [E0, 1])
        vmat = sb("vmat", [E0, P])
        vrow = sb("vrow", [P, ACT0])
        z_add = sb("z_add", [P, NT, Z0N])
        rs1 = sb("rs1", [P, H1N])

        x_sb = sb("x_sb", [P, 4, D])
        c0_hi = sb("c0_hi", [P, 2, D], f32r)
        c0_lo = sb("c0_lo", [P, 2, D], f32r)
        z0 = sb("z0", [P, Z0N])
        z0_nmax = sb("z0_nmax", [P, 1])
        z0_exp = sb("z0_exp", [P, ACT0])
        z0_sum = sb("z0_sum", [P, 1])
        z0_rec = sb("z0_rec", [P, 1])
        alpha = sb("alpha", [P, ACT0])
        g0 = sb("g0", [P, L0N])
        g0s = sb("g0s", [P, K0])
        g0t = sb("g0t", [K0, P], f32r)
        x1 = sb("x1", [P, 4, NPH, NQP])
        win = sb("win", [KIM, 2, CG, NQ])
        c1 = sb("c1", [P, D])
        c1_hi = sb("c1_hi", [P, 2, NPH, P], f32r)
        c1_lo = sb("c1_lo", [P, 2, NPH, P], f32r)
        h1 = sb("h1", [P, H1N])
        top = sb("top", [P, 8])
        top_i = sb("top_i", [P, 8], u32)
        top_f = sb("top_f", [P, 2])
        ntop = sb("ntop", [P, 1])
        t_exp = sb("t_exp", [P, 2])
        t_sum = sb("t_sum", [P, 1])
        t_rec = sb("t_rec", [P, 1])
        prob = sb("prob", [P, 2])
        gate_a = sb("gate_a", [P, E1])
        gate_b = sb("gate_b", [P, E1])
        gate = sb("gate", [P, E1])
        g1 = sb("g1", [P, 2, K1])
        g1t_hi = sb("g1t_hi", [K1, 2, P], f32r)
        g1t_lo = sb("g1t_lo", [K1, 2, P], f32r)
        y_sb = sb("y_sb", [P, 2, D])

        p_y0ab = ctx.enter_context(nc.psum_tensor("p_y0ab", [P, 2 * 512], f32))
        p_y0a, p_y0b = p_y0ab[:, 0:512], p_y0ab[:, 512:1024]
        p_c0, p_g = pb("p_c0"), pb("p_g")
        p_cv, p_c1, p_h1, p_y1 = pb("p_cv"), pb("p_c1"), pb("p_h1"), pb("p_y1")
        p_g1t = p_g[0:K1, 0:2 * P].rearrange("p (a n) -> p a n", a=2)
        NY = D // 2
        p_y0 = (p_y0a[:, Z0N:Z0N + NY], p_y0b[:, 0:NY])
        p_g0t = p_c1[0:K0, 0:P]

        ld_pack, ld_kw, ld_exp, ld_rt = sem("ld_pack"), sem("ld_kw"), sem("ld_exp"), sem("ld_rt")
        ld_act, ld_bb, ld_w0, ld_w1 = sem("ld_act"), sem("ld_bb"), sem("ld_w0"), sem("ld_w1")
        ld_a1, ld_b1, ld_wc = sem("ld_a1"), sem("ld_b1"), sem("ld_wc")
        x_loaded = [sem(f"x_loaded{n}") for n in range(4)]
        x1_stored = [sem(f"x1_stored{n}") for n in range(4)]
        win_loaded = [sem(f"win_loaded{n}") for n in range(2)]
        y_stored = [sem(f"y_stored{n}") for n in range(2)]

        zeroed_id, ident_done, ones_done, picks_zeroed = sem("zeroed_id"), sem("ident_done"), sem("ones_done"), sem("picks_zeroed")
        picks_done, iotas_done, mix_zeroed, x1_padded = sem("picks_done"), sem("iotas_done"), sem("mix_zeroed"), sem("x1_padded")
        g1_padded, lomask_0, lomask_1, lomask_2, lomask_done = sem("g1_padded"), sem("lomask_0"), sem("lomask_1"), sem("lomask_2"), sem("lomask_done")
        u1_mm, m1_done = sem("u1_mm"), sem("m1_done")
        u2_mm, m2_done = sem("u2_mm"), sem("m2_done")
        am_mm, am_done, am_max_done, am_exp_done = sem("am_mm"), sem("am_done"), sem("am_max_done"), sem("am_exp_done")
        am_rec_done, att_done, att_t_mm, att_t_done = sem("am_rec_done"), sem("att_done"), sem("att_t_mm"), sem("att_t_done")
        beta1_mm, beta1_done, beta0_mm, beta0_done = sem("beta1_mm"), sem("beta1_done"), sem("beta0_mm"), sem("beta0_done")
        kwmask_0, kwmask_1, kwmask_done = sem("kwmask_0"), sem("kwmask_1"), sem("kwmask_done")
        kw_round_done, kw_done, att_hi_done, att3_done = sem("kw_round_done"), sem("kw_done"), sem("att_hi_done"), sem("att3_done")
        mix_mm, mix_act_done, mix_dve_done = sem("mix_mm"), sem("mix_act_done"), sem("mix_dve_done")
        w0_pairs_done, w0_sum_done, w1_pairs_done, w1_sum_done = sem("w0_pairs_done"), sem("w0_sum_done"), sem("w1_pairs_done"), sem("w1_sum_done")
        a1_pairs_done, a1_sum_done, a0_sum_done = sem("a1_pairs_done"), sem("a1_sum_done"), sem("a0_sum_done")
        iota_e_done, act8_done, sel_zeroed, sel_done, sel_r_done = sem("iota_e_done"), sem("act8_done"), sem("sel_zeroed"), sem("sel_done"), sem("sel_r_done")
        a0_mm, a0_hi_done, a0_lo_done = sem("a0_mm"), sem("a0_hi_done"), sem("a0_lo_done")
        w0_hi_done, w0_lo_done = sem("w0_hi_done"), sem("w0_lo_done")
        w1_hi_done, w1_lo_done = sem("w1_hi_done"), sem("w1_lo_done")
        a1_hi_done, a1_lo_done = sem("a1_hi_done"), sem("a1_lo_done")
        b0_mm, b0_round_done, b0_done = sem("b0_mm"), sem("b0_round_done"), sem("b0_done")
        b1_mm, b1_hi_done, b1_lo_done = sem("b1_mm"), sem("b1_hi_done"), sem("b1_lo_done")
        rs0_mm, rs0_done, vlog_done, vcol2_done, vmat_done = sem("rs0_mm"), sem("rs0_done"), sem("vlog_done"), sem("vcol2_done"), sem("vmat_done")
        vrow_mm, vrow_done, z_mul_done, z_add_done = sem("vrow_mm"), sem("vrow_done"), sem("z_mul_done"), sem("z_add_done")
        rs1_mm, rs1_done = sem("rs1_mm"), sem("rs1_done")
        beta5_ones, beta5_hi, beta5_lo, beta5_done = sem("beta5_ones"), sem("beta5_hi"), sem("beta5_lo"), sem("beta5_done")
        eps_done = sem("eps_done")

        cv_mm = sem("cv_mm")
        c0_mm, c0_hi_done, c0_lo_done = sem("c0_mm"), sem("c0_hi_done"), sem("c0_lo_done")
        z0_mm, z0_done, z0_nmax_done, z0_exp_done = sem("z0_mm"), sem("z0_done"), sem("z0_nmax_done"), sem("z0_exp_done")
        z0_rec_done, alpha_done, g0_done, g0_hi_done = sem("z0_rec_done"), sem("alpha_done"), sem("g0_done"), sem("g0_hi_done")
        g0_lo_done, g0_beta_done = sem("g0_lo_done"), sem("g0_beta_done")
        g0_tr, g0t_done, y0_mm, x1_done = sem("g0_tr"), sem("g0t_done"), sem("y0_mm"), sem("x1_done")
        c1_tr, c1_hi_done, c1_lo_done = sem("c1_tr"), sem("c1_hi_done"), sem("c1_lo_done")
        h1_mm, logits_done, h1_done, top_done, top_i_done, ntop_done = sem("h1_mm"), sem("logits_done"), sem("h1_done"), sem("top_done"), sem("top_i_done"), sem("ntop_done")
        top_f_done, t_exp_done, t_rec_done, prob_done = sem("top_f_done"), sem("t_exp_done"), sem("t_rec_done"), sem("prob_done")
        gate_a_done, gate_b_done, gate_done, g1_done, g1_beta_done = sem("gate_a_done"), sem("gate_b_done"), sem("gate_done"), sem("g1_done"), sem("g1_beta_done")
        g1_tr, g1t_hi_done, g1t_lo_done = sem("g1_tr"), sem("g1t_hi_done"), sem("g1t_lo_done")
        y1_mm, y_done = sem("y1_mm"), sem("y_done")

        x_v = x.rearrange("(t b) c h -> t (b c) h", b=BT)
        out_v = out.rearrange("(t b) c h -> t (b c) h", b=BT)
        windows = scratch.rearrange("t (a i) f q -> t (i f) a q", i=GC)

        block = ctx.enter_context(nc.Block())

        def is_last(tile):
            return tile.i is None and tile.c == NT - 1

        def y1_bank(tile):
            return p_c0[:] if is_last(tile) else p_y1[:]

        def after(eng, semaphore, tile, ahead=0):
            t = tile + ahead
            if t.live():
                eng.wait_ge(semaphore, t.n() + 1)

        def after_dma(eng, semaphores, tile, ahead=0, count=16):
            t = tile + ahead
            if t.live():
                m = len(semaphores)
                eng.wait_ge(semaphores[t.mod(m)], (t.over(m) + 1) * count)

        p_beta1, p_beta0, p_vrow, p_rs0 = p_c1[:, 0:NT], p_cv[:, 0:NT], p_g[:, 0:ACT0], p_c1[:, 0:Z0N]
        p_rs1 = p_g[:, 0:H1N]

        def b1_bank(a):
            return (p_cv, p_h1)[a][0:K1, :]

        def by_phases(a):
            return a[:].rearrange("p (a r o) -> p a r o", r=NPH, o=GC)

        def by_group(a):
            return a.rearrange("p r (a o) -> p a r o", o=GC)

        def mix_blocks(tiles, n, b):
            rows = slice(b * CH, (b + 1) * CH)
            return (mix[rows, tiles, b * CH + n:(b + 1) * CH:BT],
                    p_y0ab[n * CH:(n + 1) * CH, :].rearrange("p (m t b) -> p t b m", b=BT, t=NT)[:, tiles, b])

        MIX_PARTS = (slice(0, UNROLL), slice(UNROLL, NT))

        @block.sync
        def _(sp):
            sp.dma_start(rt_sb[:], router).then_inc(ld_rt, 16)
            sp.dma_start(pack_sb[:], pack).then_inc(ld_pack, 16)
            sp.dma_start(act_sb[:], active).then_inc(ld_act, 16)
            sp.dma_start(kw_sb[:], kw).then_inc(ld_kw, 16)
            sp.dma_start(exp_sb[:], experts.rearrange("p (a d) -> p a d", a=2)).then_inc(ld_exp, 16)
            sp.dma_start(w0_sb[:], w0.rearrange("p (c d) -> p c d", c=HC)).then_inc(ld_w0, 16)
            sp.dma_start(x_sb[:, 0, :], x_v[0]).then_inc(x_loaded[0], 16)
            sp.dma_start(a1_sb[:], a1.rearrange("p (c n) -> p c n", c=HC)).then_inc(ld_a1, 16)
            sp.dma_start(bb_sb[:], b_base).then_inc(ld_bb, 16)
            sp.dma_start(w1_sb[:], w1.rearrange("p (c d) -> p c d", c=HC)).then_inc(ld_w1, 16)
            sp.dma_start(x_sb[:, 1, :], x_v[1]).then_inc(x_loaded[1], 16)
            sp.dma_start(b1_sb[:], b1.rearrange("p (a d) -> p a d", a=2)).then_inc(ld_b1, 16)
            sp.dma_start(wc_sb[:], wc.rearrange("k (g n) -> k g n", g=GROUPS)).then_inc(ld_wc, 16)

            def step(s):
                if (s + -1).live():
                    v = s + -1
                    after_dma(sp, x1_stored, v)
                    after(sp, cv_mm, v, -2)
                    for j in range(WIN // NPH):
                        rows = slice(j * NPH * GC, (j + 1) * NPH * GC)
                        sp.dma_start(win[rows, v.mod(2)], windows[v.n()][:, :, j:j + NQ]).then_inc(win_loaded[v.mod(2)], 16)
                if (s + 2).live() and (s.i is not None or s.c >= 0):
                    after(sp, x1_done, s, -2)
                    sp.dma_start(x_sb[:, (s + 2).mod(4), :], x_v[(s + 2).n()]).then_inc(x_loaded[(s + 2).mod(4)], 16)
                if (s + -3).live():
                    v = s + -3
                    after(sp, y_done, v)
                    sp.dma_start(out_v[v.n()], y_sb[:, v.mod(2), :]).then_inc(y_stored[v.mod(2)], 16)
                if s.live():
                    after(sp, x1_done, s)
                    sp.dma_start(scratch[s.n()], x1[:, s.mod(4)]).then_inc(x1_stored[s.mod(4)], 16)

            steps(sp, step, 0, NT + 2, 3, 6)
            for n in range(2):
                sp.wait_ge(y_stored[n], 16 * NT // 2)

        @block.gpsimd
        def _(pool):
            pool.memset(ident[:], 0.0).then_inc(zeroed_id, 1)
            pool.wait_ge(zeroed_id, 1)
            pool.affine_select(out=ident[:], in_=ident[:], compare_op=ALU.not_equal, fill=1.0, base=0,
                               pattern=[[-1, P]], channel_multiplier=1).then_inc(ident_done, 1)
            pool.iota(iota_slot[:], pattern=[[0, ACT0], [-1, R]], base=0, channel_multiplier=1).then_inc(iotas_done, 1)
            pool.iota(iota_row[:], pattern=[[0, ACT0]], base=0, channel_multiplier=1).then_inc(iotas_done, 1)
            pool.iota(iota_e_i[:], pattern=[[1, E1]], base=0, channel_multiplier=0).then_inc(iotas_done, 1)
            pool.memset(minus_lo_row[:], 0.0).then_inc(lomask_0, 1)
            pool.wait_ge(lomask_0, 1)
            pool.memset(minus_lo_row[2 * L0N:3 * L0N], -1.0).then_inc(lomask_1, 1)
            pool.wait_ge(lomask_1, 1)
            pool.affine_select(out=minus_lo_row[:], in_=minus_lo_row[:], compare_op=ALU.not_equal, fill=-1.0,
                               base=-(3 * L0N + 2), pattern=[[0, 1]], channel_multiplier=1).then_inc(lomask_2, 1)
            pool.wait_ge(lomask_2, 1)
            pool.affine_select(out=minus_lo_row[:], in_=minus_lo_row[:], compare_op=ALU.not_equal, fill=-1.0,
                               base=-(3 * L0N + 4), pattern=[[0, 1]], channel_multiplier=1).then_inc(lomask_done, 1)
            pool.memset(minus_lo_kw[:], -1.0).then_inc(kwmask_0, 1)
            pool.wait_ge(kwmask_0, 1)
            pool.affine_select(out=minus_lo_kw[:], in_=minus_lo_kw[:], compare_op=ALU.is_ge, fill=0.0,
                               base=-MK, pattern=[[0, 1]], channel_multiplier=1).then_inc(kwmask_1, 1)
            pool.wait_ge(kwmask_1, 1)
            pool.affine_select(out=minus_lo_kw[:], in_=minus_lo_kw[:], compare_op=ALU.is_ge, fill=0.0,
                               base=2 * MK - 1, pattern=[[0, 1]], channel_multiplier=-1).then_inc(kwmask_done, 1)
            pool.memset(mix[:], 0.0).then_inc(mix_zeroed, 1)
            pool.memset(g1[:, 0, HB:K1], 0.0).then_inc(g1_padded, 1)
            for f in range(2):
                pool.memset(x1[:, :, :, f * (NQP - 1):f * (NQP - 1) + 1], 0.0).then_inc(x1_padded, 1)

            def sum_chunks(loaded, w, pair, pairs_done, w_sum, sum_done):
                pool.wait_ge(loaded, 16)
                pool.tensor_tensor(pair[:], w[:, 0:2], w[:, 2:4], ALU.add).then_inc(pairs_done, 1)
                pool.wait_ge(pairs_done, 1)
                pool.tensor_tensor(w_sum[:], pair[:, 0], pair[:, 1], ALU.add).then_inc(sum_done, 1)

            pool.wait_ge(w0_hi_done, 1)
            pool.tensor_tensor(w0_lo[:, :, Z0N:Z0N + D], w0_sb[:], w0_hi[:, :, Z0N:Z0N + D].bitcast(f32),
                               ALU.subtract).then_inc(w0_lo_done, 1)
            sum_chunks(ld_w0, w0_sb, w_pair, w0_pairs_done, w0_sum, w0_sum_done)
            sum_chunks(ld_a1, a1_sb, a1_pair, a1_pairs_done, a1_sum, a1_sum_done)

            def step(s):
                if s.live():
                    if s.i is None and s.c == 0:
                        pool.wait_ge(beta5_done, 1)
                    after(pool, g0_tr, s, -1)
                    pool.tensor_copy(g0s[:, 3 * L0N:K0], beta5[:, s.n(), :]).then_inc(g0_beta_done, 1)
                if s.i is None and s.c == 0:
                    pool.wait_ge(w0_sum_done, 1)
                    sum_chunks(ld_w1, w1_sb, w_pair, w1_pairs_done, w1_sum, w1_sum_done)
                if s.i is None and s.c == 1:
                    pool.wait_ge(w1_hi_done, 1)
                    pool.tensor_tensor(w1_lo[:], w1_sb[:], w1_hi[:].bitcast(f32), ALU.subtract).then_inc(w1_lo_done, 1)
                if (s + -LAG).live():
                    v = s + -LAG
                    after(pool, c1_hi_done, v)
                    pool.tensor_tensor(by_group(c1_lo[:, v.mod(2)]), by_phases(c1),
                                       by_group(c1_hi[:, v.mod(2)].bitcast(f32)), ALU.subtract).then_inc(c1_lo_done, 1)
                    if v.i is None and v.c == 0:
                        pool.wait_ge(beta1_done, BT)
                    after(pool, g1_tr, v, -1)
                    pool.tensor_copy(g1[:, 1, HB:K1], beta1[:, bass.ds(v.n(), 1)]).then_inc(g1_beta_done, 1)

            steps(pool, step, 0, NT + 1, 3, 7)

        @block.scalar
        def _(act):
            act.wait_ge(eps_done, 1)
            nc.scalar.activation(vcol[:], vcol2[:], ACT.Ln).then_inc(vlog_done, 1)
            act.wait_ge(u1_mm, 1)
            nc.scalar.activation(m1[:], p_c0[:, 0:P], ACT.Gelu, bias=pack_sb[:, C_B0:C_B0 + 1]).then_inc(m1_done, 1)
            act.wait_ge(u2_mm, 1)
            nc.scalar.activation(m2[:], p_c0[:, 0:P], ACT.Gelu, bias=pack_sb[:, C_B1:C_B1 + 1]).then_inc(m2_done, 1)
            act.wait_ge(am_max_done, 1)
            nc.scalar.activation(am_exp[:], am[:], ACT.Exp, bias=am_max[:], accum_out=am_sum[:]).then_inc(am_exp_done, 1)
            act.wait_ge(ld_w0, 16)
            nc.scalar.copy(w0_hi[:, :, Z0N:Z0N + D], w0_sb[:]).then_inc(w0_hi_done, 1)
            act.wait_ge(mix_zeroed, 1)
            act.wait_ge(mix_mm, 1)
            for tiles in MIX_PARTS:
                for n in range(BT // 2):
                    for b in range(BT):
                        nc.scalar.copy(*mix_blocks(tiles, n, b)).then_inc(mix_act_done, 1)
            act.wait_ge(a0_mm, 1)
            nc.scalar.copy(w0_hi[:, :, 0:Z0N], p_h1[:, 0:HC * Z0N].rearrange("p (c n) -> p c n", c=HC)).then_inc(a0_hi_done, 1)

            def step(s):
                if (s + -LAG).live():
                    v = s + -LAG
                    after(act, c1_tr, v)
                    after(act, y1_mm, v, -2)
                    nc.scalar.copy(by_group(c1_hi[:, v.mod(2)]), by_phases(c1)).then_inc(c1_hi_done, 1)
                if s.live():
                    after(act, z0_nmax_done, s)
                    nc.scalar.activation(z0_exp[:], z0[:, L0N:Z0N], ACT.Exp, bias=z0_nmax[:],
                                         accum_out=z0_sum[:]).then_inc(z0_exp_done, 1)
                if (s + 1).live():
                    t = s + 1
                    after(act, c0_mm, t)
                    nc.scalar.copy(c0_hi[:, t.mod(2), :], p_c0[:]).then_inc(c0_hi_done, 1)
                if s.i is None and s.c == 0:
                    act.wait_ge(b0_mm, 1)
                    nc.scalar.copy(b0_round[:], p_y1[0:K0, :]).then_inc(b0_round_done, 1)
                if (s + -3).live():
                    after(act, g1_tr, s, -3)
                    nc.scalar.copy(g1t_hi[:], p_g1t).then_inc(g1t_hi_done, 1)
                if s.live():
                    after(act, g0_tr, s)
                    nc.scalar.copy(g0t[:], p_g0t).then_inc(g0t_done, 1)
                if s.i is None and s.c == -1:
                    act.wait_ge(ld_a1, 16)
                    nc.scalar.copy(a1_hi[:], a1_sb[:]).then_inc(a1_hi_done, 1)
                    act.wait_ge(ld_w1, 16)
                    nc.scalar.copy(w1_hi[:], w1_sb[:]).then_inc(w1_hi_done, 1)
                if s.i is None and s.c in (0, 1):
                    act.wait_ge(b1_mm, s.c + 1)
                    nc.scalar.copy(b1_hi[:, s.c, :], b1_bank(s.c)).then_inc(b1_hi_done, 1)
                if (s + -LAG).live():
                    after(act, ntop_done, s, -LAG)
                    nc.scalar.activation(t_exp[:], top[:, 0:2], ACT.Exp, bias=ntop[:],
                                         accum_out=t_sum[:]).then_inc(t_exp_done, 1)

            steps(act, step, -1, NT + 2, 3, 7)

        @block.vector
        def _(dve):
            V = nc.vector
            V.memset(ones[:], 1.0).then_inc(ones_done, 1)
            V.memset(pick_rs0[:], 0.0).then_inc(picks_zeroed, 1)
            V.memset(pick_bias[:], 0.0).then_inc(picks_zeroed, 1)
            V.memset(pick_rs1[:], 0.0).then_inc(picks_zeroed, 1)
            V.memset(sel[:], 0.0).then_inc(sel_zeroed, 1)
            dve.wait_ge(picks_zeroed, 3)
            V.memset(pick_rs0[:, 3 * L0N:3 * L0N + 3], 1.0).then_inc(picks_done, 1)
            V.memset(pick_bias[:, 3 * L0N + 3:K0], 1.0).then_inc(picks_done, 1)
            V.memset(pick_rs1[:, HB:K1], 1.0).then_inc(picks_done, 1)
            V.memset(beta5[:, :, 3:5], 1.0).then_inc(beta5_ones, 1)
            dve.wait_ge(ld_rt, 16)
            V.tensor_scalar(vcol2[:], rt_sb[:, D + 1:D + 2], EPS, None, ALU.add).then_inc(eps_done, 1)
            dve.wait_ge(ld_act, 16)
            dve.wait_ge(iotas_done, 3)
            V.tensor_scalar(act8[:], act_sb[:], float(R), None, ALU.mult).then_inc(act8_done, 1)
            V.tensor_copy(iota_e[:], iota_e_i[:]).then_inc(iota_e_done, 1)
            V.tensor_tensor(sel_r[:], iota_row[:], act_sb[0:E0, :], ALU.is_equal).then_inc(sel_r_done, 1)
            dve.wait_ge(act8_done, 1)
            dve.wait_ge(sel_zeroed, 1)
            for n in range(3):
                V.tensor_tensor(sel[:, n * L0N:(n + 1) * L0N].rearrange("p (s r) -> p s r", r=R), iota_slot[:],
                                act8[:].unsqueeze(2).to_broadcast([P, ACT0, R]), ALU.is_equal).then_inc(sel_done, 1)
            dve.wait_ge(ld_kw, 16)
            V.tensor_copy(kw_round[:], kw_sb[:]).then_inc(kw_round_done, 1)
            dve.wait_ge(kw_round_done, 1)
            dve.wait_ge(kwmask_done, 1)
            V.scalar_tensor_tensor(kw_stack[:], kw_round[:].bitcast(f32), minus_lo_kw[0:KM], kw_sb[:],
                                   ALU.mult, ALU.add).then_inc(kw_done, 1)
            dve.wait_ge(am_mm, 1)
            V.tensor_tensor(am[:], p_g[:, 0:MK], pack_sb[:, C_B2:C_B2 + MK], ALU.add).then_inc(am_done, 1)
            dve.wait_ge(am_done, 1)
            V.tensor_reduce(am_max[:], am[:], X, ALU.max, negate=True).then_inc(am_max_done, 1)
            dve.wait_ge(beta1_mm, 1)
            V.tensor_scalar(beta1[:], p_beta1, pack_sb[:, C_FS:C_FS + 1], None, ALU.add).then_inc(beta1_done, BT)
            dve.wait_ge(am_exp_done, 1)
            V.reciprocal(am_rec[:], am_sum[:]).then_inc(am_rec_done, 1)
            dve.wait_ge(am_rec_done, 1)
            V.tensor_scalar(att3[:, 0:2].bitcast(f32r), am_exp[:].unsqueeze(1).to_broadcast([P, 2, MK]), am_rec[:], None,
                            ALU.mult).then_inc(att_hi_done, 1)
            V.tensor_scalar(att[:], am_exp[:], am_rec[:], None, ALU.mult).then_inc(att_done, 1)
            dve.wait_ge(att_hi_done, 1)
            dve.wait_ge(att_done, 1)
            V.tensor_tensor(att3[:, 2], att[:], att3[:, 0], ALU.subtract).then_inc(att3_done, 1)
            dve.wait_ge(att_t_mm, 1)
            V.tensor_copy(att_t[:], p_g[0:KM, 0:BATCH]).then_inc(att_t_done, 1)
            dve.wait_ge(vlog_done, 1)
            V.tensor_tensor(vmat[:, 0:1], vcol[:], rt_sb[:, D:D + 1], ALU.add).then_inc(vcol2_done, 1)
            dve.wait_ge(vcol2_done, 1)
            V.tensor_copy(vmat[:, 1:P], vmat[:, 0:1].to_broadcast([E0, P - 1])).then_inc(vmat_done, 1)
            dve.wait_ge(mix_zeroed, 1)
            dve.wait_ge(mix_mm, 1)
            for tiles in MIX_PARTS:
                for n in range(BT // 2, BT):
                    for b in range(BT):
                        V.tensor_copy(*mix_blocks(tiles, n, b)).then_inc(mix_dve_done, 1)
            dve.wait_ge(a0_mm, 1)
            dve.wait_ge(a0_hi_done, 1)
            V.tensor_reduce(a0_sum[:], p_h1[:, 0:HC * Z0N].rearrange("p (c n) -> p n c", c=HC), X, ALU.add).then_inc(a0_sum_done, 1)
            V.tensor_tensor(w0_lo[:, :, 0:Z0N], p_h1[:, 0:HC * Z0N].rearrange("p (c n) -> p c n", c=HC),
                            w0_hi[:, :, 0:Z0N].bitcast(f32), ALU.subtract).then_inc(a0_lo_done, 1)
            dve.wait_ge(beta0_mm, 1)
            V.tensor_copy(beta0[:], p_beta0).then_inc(beta0_done, 1)
            dve.wait_ge(beta0_done, 1)
            V.tensor_copy(beta5[:, :, 0].bitcast(f32r), beta0[:]).then_inc(beta5_hi, 1)
            dve.wait_ge(beta5_hi, 1)
            V.tensor_tensor(beta5[:, :, 1], beta0[:], beta5[:, :, 0], ALU.subtract).then_inc(beta5_lo, 1)
            dve.wait_ge(beta5_lo, 1)
            dve.wait_ge(beta5_ones, 1)
            V.tensor_copy(beta5[:, :, 2], beta5[:, :, 0]).then_inc(beta5_done, 1)

            def step(s):
                def output(v):
                    after(dve, y1_mm, v)
                    after_dma(dve, y_stored, v, -2)
                    V.tensor_tensor(y_sb[:, v.mod(2), :].rearrange("p (q f) -> p f q", f=NPH),
                                    y1_bank(v).rearrange("p (f q) -> p f q", f=NPH), x1[:, v.mod(4), :, 1:1 + NQ],
                                    ALU.add).then_inc(y_done, 1)

                if (s + -LAG).live():
                    v = s + -LAG
                    after(dve, cv_mm, v)
                    after(dve, c1_hi_done, v, -1)
                    after(dve, c1_lo_done, v, -1)
                    V.transpose(c1[:], p_cv[:]).then_inc(c1_tr, 1)
                if s.live():
                    after(dve, z0_mm, s)
                    if s.i is None and s.c == 0:
                        dve.wait_ge(z_add_done, 1)
                    V.tensor_tensor(z0[:], p_y0a[:, 0:Z0N], z_add[:, s.n(), :], ALU.add).then_inc(z0_done, 1)
                    after(dve, z0_done, s)
                    V.tensor_reduce(z0_nmax[:], z0[:, L0N:Z0N], X, ALU.max, negate=True).then_inc(z0_nmax_done, 1)
                    after(dve, z0_exp_done, s)
                    V.reciprocal(z0_rec[:], z0_sum[:]).then_inc(z0_rec_done, 1)
                    after(dve, z0_rec_done, s)
                    V.tensor_scalar(alpha[:], z0_exp[:], z0_rec[:], SCALING, ALU.mult, ALU.mult).then_inc(alpha_done, 1)
                    after(dve, alpha_done, s)
                    V.tensor_tensor(g0[:].rearrange("p (s r) -> p s r", r=R), z0[:, 0:L0N].rearrange("p (s r) -> p s r", r=R),
                                    alpha[:].unsqueeze(2).to_broadcast([P, ACT0, R]), ALU.mult).then_inc(g0_done, 1)
                    after(dve, g0_done, s)
                    after(dve, g0_tr, s, -1)
                    V.tensor_copy(g0s[:, 0:3 * L0N].rearrange("p (a n) -> p a n", n=L0N)[:, 0:3:2, :].bitcast(f32r),
                                  g0[:].unsqueeze(1).to_broadcast([P, 2, L0N])).then_inc(g0_hi_done, 1)
                    after(dve, g0_hi_done, s)
                    V.tensor_tensor(g0s[:, L0N:2 * L0N], g0[:], g0s[:, 0:L0N], ALU.subtract).then_inc(g0_lo_done, 1)
                if (s + 1).live():
                    t = s + 1
                    after(dve, c0_hi_done, t)
                    V.tensor_tensor(c0_lo[:, t.mod(2), :], p_c0[:], c0_hi[:, t.mod(2), :].bitcast(f32),
                                    ALU.subtract).then_inc(c0_lo_done, 1)
                if s.i is None and s.c == 0:
                    dve.wait_ge(b0_round_done, 1)
                    dve.wait_ge(lomask_done, 1)
                    V.scalar_tensor_tensor(b0_stack[:], b0_round[:].bitcast(f32), minus_lo_row[0:K0], p_y1[0:K0, :],
                                           ALU.mult, ALU.add).then_inc(b0_done, 1)
                if (s + -3).live():
                    after(dve, g1t_hi_done, s, -3)
                    V.tensor_tensor(g1t_lo[:], p_g1t, g1t_hi[:].bitcast(f32), ALU.subtract).then_inc(g1t_lo_done, 1)
                if (s + -3).live() and not is_last(s + -LAG):
                    output(s + -3)
                if s.live():
                    after(dve, y0_mm, s)
                    after_dma(dve, x1_stored, s, -4)
                    for n in range(2):
                        phases = slice(n * NPH // 2, (n + 1) * NPH // 2)
                        last = V.tensor_tensor(x1[:, s.mod(4), phases, 1:1 + NQ], p_y0[n].rearrange("p (f q) -> p f q", q=NQ),
                                               x_sb[:, s.mod(4), :].rearrange("p (q f) -> p f q", f=NPH)[:, phases, :], ALU.add)
                    last.then_inc(x1_done, 1)
                if s.i is None and s.c == -1:
                    dve.wait_ge(rs0_mm, 1)
                    V.tensor_copy(rs0[:], p_rs0).then_inc(rs0_done, 1)
                    dve.wait_ge(rs0_done, 1)
                    V.tensor_tensor(z_add[:], rs0[:].unsqueeze(1).to_broadcast([P, NT, Z0N]),
                                    beta0[:].unsqueeze(2).to_broadcast([P, NT, Z0N]), ALU.mult).then_inc(z_mul_done, 1)
                    dve.wait_ge(vrow_mm, 1)
                    V.tensor_copy(vrow[:], p_vrow).then_inc(vrow_done, 1)
                    dve.wait_ge(z_mul_done, 1)
                    dve.wait_ge(vrow_done, 1)
                    V.tensor_tensor(z_add[:, :, L0N:Z0N], z_add[:, :, L0N:Z0N],
                                    vrow[:].unsqueeze(1).to_broadcast([P, NT, ACT0]), ALU.add).then_inc(z_add_done, 1)
                    dve.wait_ge(a1_hi_done, 1)
                    V.tensor_tensor(a1_lo[:], a1_sb[:], a1_hi[:].bitcast(f32), ALU.subtract).then_inc(a1_lo_done, 1)
                if s.i is None and s.c == 0:
                    dve.wait_ge(rs1_mm, 1)
                    V.tensor_copy(rs1[:], p_rs1).then_inc(rs1_done, 1)
                if s.i is None and s.c in (0, 1):
                    dve.wait_ge(b1_hi_done, s.c + 1)
                    V.tensor_tensor(b1_lo[:, s.c, :], b1_bank(s.c), b1_hi[:, s.c, :].bitcast(f32), ALU.subtract).then_inc(b1_lo_done, 1)
                if (s + -LAG).live():
                    v = s + -LAG
                    after(dve, h1_mm, v)
                    if v.i is None and v.c == 0:
                        dve.wait_ge(rs1_done, 1)
                        dve.wait_ge(beta1_done, BT)
                        dve.wait_ge(iota_e_done, 1)
                    beta = beta1[:, bass.ds(v.n(), 1)]
                    V.scalar_tensor_tensor(h1[:, L1N:H1N], rs1[:, L1N:H1N], beta, p_h1[:, L1N:H1N],
                                           ALU.mult, ALU.add).then_inc(logits_done, 1)
                    after(dve, logits_done, v)
                    V.scalar_tensor_tensor(h1[:, 0:L1N], rs1[:, 0:L1N], beta, p_h1[:, 0:L1N],
                                           ALU.mult, ALU.add).then_inc(h1_done, 1)
                    V.max(top[:], h1[:, L1N:H1N]).then_inc(top_done, 1)
                    after(dve, top_done, v)
                    V.tensor_scalar(ntop[:], top[:, 0:1], -1.0, None, ALU.mult).then_inc(ntop_done, 1)
                    V.max_index(top_i[:], top[:], h1[:, L1N:H1N]).then_inc(top_i_done, 1)
                    after(dve, top_i_done, v)
                    V.tensor_copy(top_f[:], top_i[:, 0:2]).then_inc(top_f_done, 1)
                    after(dve, t_exp_done, v)
                    V.reciprocal(t_rec[:], t_sum[:]).then_inc(t_rec_done, 1)
                    after(dve, t_rec_done, v)
                    V.tensor_scalar(prob[:], t_exp[:], t_rec[:], SCALING, ALU.mult, ALU.mult).then_inc(prob_done, 1)
                    after(dve, prob_done, v)
                    after(dve, top_f_done, v)
                    V.tensor_scalar(gate_a[:], iota_e[:], top_f[:, 0:1], prob[:, 0:1], ALU.is_equal, ALU.mult).then_inc(gate_a_done, 1)
                    V.tensor_scalar(gate_b[:], iota_e[:], top_f[:, 1:2], prob[:, 1:2], ALU.is_equal, ALU.mult).then_inc(gate_b_done, 1)
                    after(dve, gate_a_done, v)
                    after(dve, gate_b_done, v)
                    V.tensor_tensor(gate[:], gate_a[:], gate_b[:], ALU.add).then_inc(gate_done, 1)
                    after(dve, gate_done, v)
                    after(dve, h1_done, v)
                    after(dve, g1_tr, v, -1)
                    V.tensor_tensor(g1[:, :, 0:HB].rearrange("p a (e r) -> p a e r", r=R),
                                    h1[:, 0:L1N].rearrange("p (a e r) -> p a e r", a=2, r=R),
                                    gate[:].rearrange("p (a e) -> p a e", a=2).unsqueeze(3).to_broadcast([P, 2, E1 // 2, R]),
                                    ALU.mult).then_inc(g1_done, 1)
                if is_last(s + -LAG):
                    output(s + -3)

            dve.wait_ge(x1_padded, 2)
            steps(dve, step, -1, NT + 2, 3, 7)

        @block.tensor
        def _(pe):
            mm = nc.tensor.matmul

            def hi_passes(psum, operands, start):
                for n, (lhs_hi, _, rhs_hi, rhs_lo) in enumerate(operands):
                    mm(psum, lhs_hi, rhs_hi, start=start and n == 0, stop=False)
                    mm(psum, lhs_hi, rhs_lo, start=False, stop=False)

            def lo_passes(psum, operands, stop):
                for n, (_, lhs_lo, rhs_hi, _) in enumerate(operands):
                    last = mm(psum, lhs_lo, rhs_hi, start=False, stop=stop and n == len(operands) - 1)
                return last

            def active_rows(chunks):
                for c in chunks:
                    mm(p_h1[:, c * Z0N:c * Z0N + L0N], exp_sb[:, 0, c * P:(c + 1) * P], sel[:, 0:L0N], start=True, stop=True)
                    last = mm(p_h1[:, c * Z0N + L0N:(c + 1) * Z0N], rt_sb[:, c * P:(c + 1) * P], sel_r[:], start=True, stop=True)
                return last

            pe.wait_ge(ld_pack, 16)
            cond = pack_sb[:, C_COND:C_COND + BATCH]
            mm(p_c0[:, 0:P], pack_sb[:, C_W0:C_W0 + P], cond, start=True, stop=True).then_inc(u1_mm, 1)
            by_batch = [slice(b * CH, (b + 1) * CH) for b in range(BT)]
            for b in range(BT):
                last = mm(p_beta1[by_batch[b]], pack_sb[:, C_CW:C_CW + CH],
                          cond.rearrange("p (t b) -> p b t", b=BT)[:, b, :], start=True, stop=True)
            last.then_inc(beta1_mm, 1)
            pe.wait_ge(m1_done, 1)
            mm(p_c0[:, 0:P], pack_sb[:, C_W1:C_W1 + P], m1[:], start=True, stop=True).then_inc(u2_mm, 1)
            pe.wait_ge(m2_done, 1)
            mm(p_g[:, 0:MK], m2[:], pack_sb[:, C_W2:C_W2 + MK], start=True, stop=True).then_inc(am_mm, 1)
            pe.wait_ge(sel_done, 3)
            pe.wait_ge(sel_r_done, 1)
            pe.wait_ge(ld_exp, 16)
            pe.wait_ge(ld_rt, 16)
            active_rows(range(HC // 2))
            pe.wait_ge(ident_done, 1)
            pe.wait_ge(att3_done, 1)
            nc.tensor.transpose(p_g[0:KM, 0:BATCH], att3[:].rearrange("p a k -> p (a k)"), ident[:]).then_inc(att_t_mm, 1)
            pe.wait_ge(kw_done, 1)
            pe.wait_ge(att_t_done, 1)
            for m in range(CH // BT):
                last = mm(p_y0ab[:, m * BATCH:(m + 1) * BATCH], kw_stack[:, m * BT * CH:(m + 1) * BT * CH], att_t[:],
                          start=True, stop=True)
            last.then_inc(mix_mm, 1)
            for b in range(BT):
                last = mm(p_beta0[by_batch[b]], kw_stack[:, CH * CH:CH * CH + CH].bitcast(f32),
                          att_t[:].bitcast(f32).rearrange("k (t b) -> k b t", b=BT)[:, b, :], start=True, stop=True)
            last.then_inc(beta0_mm, 1)
            active_rows(range(HC // 2, HC)).then_inc(a0_mm, 1)
            pe.wait_ge(vmat_done, 1)
            mm(p_vrow, vmat[:], sel_r[:], start=True, stop=True).then_inc(vrow_mm, 1)

            def step(s):
                c0_pairs = [(c0_hi[:, s.mod(2), c * P:(c + 1) * P], c0_lo[:, s.mod(2), c * P:(c + 1) * P]) for c in range(HC)]

                def other_half():
                    other = [(*c0_pairs[c], w0_hi[:, c, Z0N + NY:Z0N + D], w0_lo[:, c, Z0N + NY:Z0N + D]) for c in range(HC)]
                    hi_passes(p_y0[1], other, True)
                    lo_passes(p_y0[1], other, False)

                def conv(v):
                    after_dma(pe, win_loaded, v, 0, 16 * (WIN // NPH))
                    after(pe, c1_tr, v, -1)
                    if v.i is None and v.c == 0:
                        pe.wait_ge(ld_wc, 16)
                        pe.wait_ge(b1_hi_done, 1)
                        pe.wait_ge(b1_lo_done, 1)
                    for g in range(GROUPS):
                        for j in range(P // CH):
                            rows = slice(j * CH, (j + 1) * CH)
                            last = mm(p_cv[rows, :].rearrange("p (b g m) -> p b g m", b=BT, g=GROUPS)[:, :, g], wc_sb[:, g, :],
                                      win[:, v.mod(2)].rearrange("p (b g) q -> p b g q", g=GROUPS)[:, :, g, rows],
                                      start=True, stop=True)
                    last.then_inc(cv_mm, 1)

                def transpose_g1(v):
                    after(pe, g1_done, v)
                    after(pe, g1_beta_done, v)
                    after(pe, g1t_lo_done, v, -1)
                    if v.i is None and v.c == 0:
                        pe.wait_ge(g1_padded, 1)
                        pe.wait_ge(rs1_done, 1)
                    for a in range(2):
                        last = nc.tensor.transpose(p_g1t[:, a, :], g1[:, a, :], ident[:])
                    last.then_inc(g1_tr, 1)

                def low_rank_1(v):
                    ranks = [(g1t_hi[:, a, :], g1t_lo[:, a, :], b1_hi[:, a, :], b1_lo[:, a, :]) for a in range(2)]
                    after(pe, g1t_hi_done, v)
                    hi_passes(y1_bank(v), ranks, False)
                    after(pe, g1t_lo_done, v)
                    lo_passes(y1_bank(v), ranks, True).then_inc(y1_mm, 1)

                def lows_1(v):
                    lows = [(c1_hi[:, v.mod(2), c, :], c1_lo[:, v.mod(2), c, :], a1_hi[:, c, :], a1_lo[:, c, :]) for c in range(HC)]
                    after(pe, c1_hi_done, v)
                    after(pe, h1_done, v, -1)
                    if v.i is None and v.c == 0:
                        pe.wait_ge(a1_lo_done, 1)
                        pe.wait_ge(b1_hi_done, 2)
                        pe.wait_ge(b1_lo_done, 2)
                    hi_passes(p_h1[:, 0:H1N], lows, True)
                    after(pe, c1_lo_done, v)
                    lo_passes(p_h1[:, 0:H1N], lows, True).then_inc(h1_mm, 1)

                def base_1(v, between=lambda: None):
                    full = [(c1_hi[:, v.mod(2), c, :], c1_lo[:, v.mod(2), c, :], w1_hi[:, c, :], w1_lo[:, c, :]) for c in range(HC)]
                    if v.i is None and v.c == 0:
                        pe.wait_ge(b0_done, 1)
                        pe.wait_ge(w1_lo_done, 1)
                    elif not is_last(v):
                        after(pe, y_done, v, -1)
                    else:
                        after(pe, c0_lo_done, v)
                    hi_passes(y1_bank(v), full, True)
                    between()
                    lo_passes(y1_bank(v), full, False)

                if s.live():
                    after(pe, c0_lo_done, s)
                if s.i is None and s.c == 0:
                    pe.wait_ge(w0_lo_done, 1)
                    pe.wait_ge(mix_act_done, BT * BT)
                    pe.wait_ge(mix_dve_done, BT * BT)
                    pe.wait_ge(a0_lo_done, 1)
                if s.live():
                    after(pe, x1_done, s, -1)
                    first = [(*c0_pairs[c], w0_hi[:, c, 0:Z0N + NY], w0_lo[:, c, 0:Z0N + NY]) for c in range(HC)]
                    hi_passes(p_y0a[:, 0:Z0N + NY], first, True)
                    lo_passes(p_y0a[:, 0:Z0N + NY], first, True).then_inc(z0_mm, 1)
                if (s + 1).live():
                    t = s + 1
                    after_dma(pe, x_loaded, t)
                    if t.i is None and t.c in (0, 1):
                        pe.wait_ge(mix_act_done, (t.c + 1) * BT * BT // 2)
                        pe.wait_ge(mix_dve_done, (t.c + 1) * BT * BT // 2)
                    after(pe, c0_lo_done, s)
                    for c in range(HC):
                        cols = slice(c * P, (c + 1) * P)
                        last = mm(p_c0[:, cols], x_sb[:, t.mod(4), cols], mix[:, t.n(), :], start=True, stop=True)
                    last.then_inc(c0_mm, 1)
                if s.i is None and s.c == -1:
                    pe.wait_ge(ones_done, 1)
                    pe.wait_ge(a0_sum_done, 1)
                    pe.wait_ge(beta1_done, BT)
                    mm(p_rs0, ones[:], a0_sum[:], start=True, stop=True).then_inc(rs0_mm, 1)
                    mm(p_y1[0:K0, :], sel[:], exp_sb[:, 1, :], start=True, stop=False)
                if s.i is None and s.c == 0:
                    pe.wait_ge(w0_sum_done, 1)
                    pe.wait_ge(picks_done, 3)
                    pe.wait_ge(ld_bb, 16)
                    mm(p_y1[0:K0, :], pick_rs0[:], w0_sum[:], start=False, stop=False)
                    mm(p_y1[0:K0, :], pick_bias[:], bb_sb[:], start=False, stop=True).then_inc(b0_mm, 1)
                if (s + -3).live() and not is_last(s + -3):
                    transpose_g1(s + -3)
                lows_early = s.i is None and s.c == LAG
                if s.live():
                    other_half()
                if lows_early:
                    lows_1(s + -LAG)
                if s.live():
                    after(pe, g0_lo_done, s)
                    after(pe, g0_beta_done, s)
                    if s.i is None and s.c == 0:
                        pe.wait_ge(rs0_done, 1)
                    nc.tensor.transpose(p_g0t, g0s[:], ident[:]).then_inc(g0_tr, 1)
                if (s + -LAG).live() and is_last(s + -LAG):
                    lows_1(s + -LAG)
                    low_rank_1(s + -3)
                    base_1(s + -LAG, lambda: transpose_g1(s + -LAG))
                elif (s + -3).live():
                    low_rank_1(s + -3)
                if s.i is None and s.c == 0:
                    pe.wait_ge(a1_sum_done, 1)
                    pe.wait_ge(vrow_done, 1)
                    mm(p_rs1, ones[:], a1_sum[:], start=True, stop=True).then_inc(rs1_mm, 1)
                if s.live():
                    after(pe, g0t_done, s)
                    if s.i is None and s.c == 0:
                        pe.wait_ge(b0_done, 1)
                    mm(p_y0[0], g0t[:], b0_stack[:, 0:NY], start=False, stop=True, skip_group_check=True)
                    last = mm(p_y0[1], g0t[:], b0_stack[:, NY:D], start=False, stop=True)
                    last.then_inc(y0_mm, 1)
                if s.i is None and s.c == 0:
                    pe.wait_ge(ld_b1, 16)
                    pe.wait_ge(beta0_done, 1)
                    mm(b1_bank(0), ident[0:HB, 0:K1], b1_sb[:, 0, :], start=True, stop=True).then_inc(b1_mm, 1)
                if s.i is None and s.c == 1:
                    pe.wait_ge(w1_sum_done, 1)
                    mm(b1_bank(1), ident[0:HB, 0:K1], b1_sb[:, 1, :], start=True, stop=False)
                    mm(b1_bank(1), pick_rs1[:], w1_sum[:], start=False, stop=True).then_inc(b1_mm, 1)
                if (s + -LAG).live() and not is_last(s + -LAG) and not lows_early:
                    lows_1(s + -LAG)
                conv_early = s.i is None and s.c >= NT - 1
                if (s + -1).live() and conv_early:
                    conv(s + -1)
                if (s + -LAG).live() and not is_last(s + -LAG):
                    base_1(s + -LAG)
                if (s + -1).live() and not conv_early:
                    conv(s + -1)

            steps(pe, step, -1, NT + 2, 3, 7)


def by_phase(a):
    return np.ascontiguousarray(a.reshape(*a.shape[:-1], NQ, NPH).swapaxes(-1, -2)).reshape(a.shape)


def lay_out(i):
    f = np.float32
    pack = np.zeros((P, C_END), f)
    pack[:, C_COND:C_COND + BATCH] = i["cond_128"].T
    pack[:, C_W0:C_W0 + P] = i["L0_cond_W0"]
    pack[:, C_W1:C_W1 + P] = i["L0_cond_W1"]
    pack[:, C_W2:C_W2 + MK] = i["L0_cond_W2"]
    pack[:, C_B2:C_B2 + MK] = i["L0_cond_b2"][None, :]
    pack[:, C_B0] = i["L0_cond_b0"]
    pack[:, C_B1] = i["L0_cond_b1"]
    pack[:, C_FS] = np.tile(i["fside_S_0"], BT)
    pack[:, C_CW:C_CW + CH] = i["L1_cond_c_weight"].T
    kw = np.tile(np.concatenate([i["L0_cond_weight"].reshape(MK, CH * CH), i["L0_cond_bias_k"]], 1), (3, 1))
    experts = np.stack([i["L0_ffn_lora_A"].reshape(P, D),
                        by_phase(i["L0_ffn_lora_B"].transpose(0, 2, 1).reshape(P, D))], 1)
    router = np.concatenate([i["L0_ffn_router_W"], i["L0_ffn_router_b"][:, None], i["L0_ffn_domain_prior"][:, None]], 1)
    w0 = by_phase(i["L0_ffn_W_base"].T).reshape(HC, P, D).transpose(1, 0, 2)
    w1 = by_phase(i["L1_ffn_base_W"].T).reshape(NQ, NPH * D)
    a1 = np.concatenate([i["L1_ffn_lora_A"].reshape(L1N, D), i["L1_ffn_gate_W"]], 0).T.reshape(NQ, NPH * H1N)
    b1 = by_phase(i["L1_ffn_lora_B"].transpose(0, 2, 1).reshape(L1N, D)).reshape(2, HB, D).transpose(1, 0, 2)
    wc = np.zeros((WIN // NPH, GC, NPH, GROUPS, NPH, GC), f)
    w = i["L1_cond_weight"].reshape(GROUPS, GC, GC, TAPS)
    for s in range(WIN):
        for r in range(NPH):
            if 0 <= s - r < TAPS:
                wc[s // NPH, :, s % NPH, :, r, :] = w[:, :, :, s - r].transpose(2, 0, 1)
    c = np.ascontiguousarray
    return {
        "x": c(i["x"]), "pack": pack, "kw": c(kw), "experts": c(experts.reshape(P, -1)),
        "router": c(router), "active": c(np.broadcast_to(i["L0_ffn_active"], (P, ACT0))),
        "b_base": c(by_phase(i["L0_ffn_b_base"])[None, :]), "w0": c(w0.reshape(P, -1)), "w1": c(w1), "a1": c(a1),
        "b1": c(b1.reshape(HB, -1)), "wc": c(wc.reshape(KIM, -1)),
    }


def kernel(**inputs):
    import concourse.bacc as bacc
    from concourse.bass_utils import run_bass_kernel_spmd

    arrays = lay_out({k: np.asarray(v) for k, v in inputs.items()})
    nc = bacc.Bacc("TRN2", target_bir_lowering=False, num_devices=1)
    args = {n: nc.dram_tensor(f"in_{n}", a.shape, mybir.dt.from_np(a.dtype), kind="ExternalInput").ap()
            for n, a in arrays.items()}
    out = nc.dram_tensor("out", (BATCH, CH, D), mybir.dt.float32, kind="ExternalOutput").ap()
    build(nc, out=out, **args)
    r = run_bass_kernel_spmd(nc, [{f"in_{n}": a for n, a in arrays.items()}], core_ids=[0])
    return r.results[0]["out"]
```
